# Optimizing a Trainium2 kernel written in Bass

```python
import numpy as np
import jax
import jax.numpy as jnp

def _softmax(x, axis=-1):
    return jax.nn.softmax(x, axis=axis)

def _gelu(x):
    return jax.nn.gelu(x, approximate=True)

def _silu(x):
    return jax.nn.silu(x)

def _sigmoid(x):
    return jax.nn.sigmoid(x)

def _layernorm(x, axis=-1, eps=1e-05):
    m = jnp.mean(x, axis=axis, keepdims=True)
    v = jnp.var(x, axis=axis, keepdims=True)
    return (x - m) / jnp.sqrt(v + eps)

def _scatter_add(tgt, idx, src, axis=0):
    return tgt.at[idx].add(src)

def _segment_sum(src, seg, n):
    return jax.ops.segment_sum(src, seg, n)
kernel_name = 'mk_xattn_ffn_d1_seqx_r4_d75e9c'

def setup_inputs(seed: int=0):
    np.random.seed(seed)
    _w = jnp.asarray

    def _rec_inputs():
        import jax
        import jax.numpy as jnp
        _rk = jax.random.key(seed)
        x = 7.22e-05 + 1 * jax.random.normal(jax.random.fold_in(_rk, 1), (16, 128, 1024), jnp.float32)
        _lenS = 128 - jax.random.randint(jax.random.fold_in(_rk, 7), (16,), 0, max(1, 128 // 4) + 1, jnp.int32)
        _lenS2 = 128 - jax.random.randint(jax.random.fold_in(_rk, 8), (16,), 0, max(1, 128 // 4) + 1, jnp.int32)
        _ctx_4096P = jax.random.normal(jax.random.fold_in(_rk, 11), (16, 16, 1024), jnp.float32)
        _ctx_4096c = jax.random.dirichlet(jax.random.fold_in(_rk, 511), 0.3 * jnp.ones((16,), jnp.float32), (16, 128))
        _ctx_4096t = jnp.einsum('bsk,bkd->bsd', _ctx_4096c, _ctx_4096P)
        _ctx_4096t = _ctx_4096t * jax.lax.rsqrt(jnp.mean(jnp.square(_ctx_4096t)) + 1e-12) * 0.953939
        ctx_4096 = 4.13588e-05 + 0.999923 * (_ctx_4096t + 0.3 * jax.random.normal(jax.random.fold_in(_rk, 611), (16, 128, 1024), jnp.float32))
        return (x, ctx_4096)
    x, ctx_4096 = _rec_inputs()

    def _L0_xattn_setup():
        import jax, jax.numpy as jnp
        import numpy as np
        import math
        D_MODEL = 256
        NHEAD = 16
        MAX_SUP = 4
        DK = D_MODEL // NHEAD
        DM = D_MODEL * MAX_SUP
        B, S = (2, 256)
        key = jax.random.key(seed)
        ks = jax.random.split(key, 12)
        std = 0.02
        inp = {'q': jax.random.normal(ks[0], (B, S, DM), jnp.float32), 'k': jax.random.normal(ks[1], (B, S, DM), jnp.float32), 'v': jax.random.normal(ks[2], (B, S, DM), jnp.float32), 'Wq': jax.random.normal(ks[3], (DM, DM), jnp.float32) * std, 'bq': jnp.zeros((DM,), jnp.float32), 'Wk': jax.random.normal(ks[4], (DM, DM), jnp.float32) * std, 'bk': jnp.zeros((DM,), jnp.float32), 'Wv': jax.random.normal(ks[5], (DM, DM), jnp.float32) * std, 'bv': jnp.zeros((DM,), jnp.float32), 'interference': jax.random.normal(ks[6], (NHEAD, MAX_SUP, MAX_SUP), jnp.float32), 'amp': jnp.ones((1,), jnp.float32), 'Wo': jax.random.normal(ks[7], (DM, DM), jnp.float32) * std, 'bo': jnp.zeros((DM,), jnp.float32)}
        return inp
    _L0_xattn_all = _L0_xattn_setup()
    _L0_xattn_in = {k: v for k, v in _L0_xattn_all.items() if k in ('Wq', 'bq', 'Wk', 'bk', 'Wv', 'bv', 'interference', 'amp', 'Wo', 'bo')}
    del _L0_xattn_all

    def _L0_ffn_setup():
        import jax, jax.numpy as jnp
        import numpy as np

        def _dequant_linear(x, wq, scale):
            w = wq.astype(jnp.float32) * scale[:, None]
            return jnp.einsum('bsh,oh->bso', x, w)
        key = jax.random.key(seed)
        ks = jax.random.split(key, 7)
        B, S, H, I = (2, 512, 1024, 3584)
        x = jax.random.normal(ks[0], (B, S, H), dtype=jnp.float32)
        gate_wq = jax.random.randint(ks[1], (I, H), -128, 128, dtype=jnp.int32)
        up_wq = jax.random.randint(ks[2], (I, H), -128, 128, dtype=jnp.int32)
        down_wq = jax.random.randint(ks[3], (H, I), -128, 128, dtype=jnp.int32)
        gate_scale = jax.random.uniform(ks[4], (I,), dtype=jnp.float32, minval=0.5, maxval=1.5) / (127.0 * np.sqrt(H))
        up_scale = jax.random.uniform(ks[5], (I,), dtype=jnp.float32, minval=0.5, maxval=1.5) / (127.0 * np.sqrt(H))
        down_scale = jax.random.uniform(ks[6], (H,), dtype=jnp.float32, minval=0.5, maxval=1.5) / (127.0 * np.sqrt(I))
        return {'x': x, 'gate_wq': gate_wq, 'gate_scale': gate_scale, 'up_wq': up_wq, 'up_scale': up_scale, 'down_wq': down_wq, 'down_scale': down_scale}
    _L0_ffn_all = _L0_ffn_setup()
    _L0_ffn_in = {k: v for k, v in _L0_ffn_all.items() if k in ('gate_wq', 'gate_scale', 'up_wq', 'up_scale', 'down_wq', 'down_scale')}
    del _L0_ffn_all
    return {'x': x, 'ctx_4096': ctx_4096, 'L0_xattn_Wq': _L0_xattn_in['Wq'], 'L0_xattn_bq': _L0_xattn_in['bq'], 'L0_xattn_Wk': _L0_xattn_in['Wk'], 'L0_xattn_bk': _L0_xattn_in['bk'], 'L0_xattn_Wv': _L0_xattn_in['Wv'], 'L0_xattn_bv': _L0_xattn_in['bv'], 'L0_xattn_interference': _L0_xattn_in['interference'], 'L0_xattn_amp': _L0_xattn_in['amp'], 'L0_xattn_Wo': _L0_xattn_in['Wo'], 'L0_xattn_bo': _L0_xattn_in['bo'], 'L0_ffn_gate_wq': _L0_ffn_in['gate_wq'], 'L0_ffn_gate_scale': _L0_ffn_in['gate_scale'], 'L0_ffn_up_wq': _L0_ffn_in['up_wq'], 'L0_ffn_up_scale': _L0_ffn_in['up_scale'], 'L0_ffn_down_wq': _L0_ffn_in['down_wq'], 'L0_ffn_down_scale': _L0_ffn_in['down_scale']}

def reference(x, ctx_4096, L0_xattn_Wq, L0_xattn_bq, L0_xattn_Wk, L0_xattn_bk, L0_xattn_Wv, L0_xattn_bv, L0_xattn_interference, L0_xattn_amp, L0_xattn_Wo, L0_xattn_bo, L0_ffn_gate_wq, L0_ffn_gate_scale, L0_ffn_up_wq, L0_ffn_up_scale, L0_ffn_down_wq, L0_ffn_down_scale):
    import jax
    import jax.numpy as jnp

    def _L0_xattn_ref(q, k, v, Wq, bq, Wk, bk, Wv, bv, interference, amp, Wo, bo):
        import jax, jax.numpy as jnp
        import numpy as np
        import math
        D_MODEL = 256
        NHEAD = 16
        MAX_SUP = 4
        DK = D_MODEL // NHEAD
        DM = D_MODEL * MAX_SUP
        B, S = (2, 256)
        b, s, dm = q.shape
        H, M = (interference.shape[0], interference.shape[1])
        dk = dm // (H * M)

        def proj(x, W, bias):
            y = x @ W.T + bias
            y = y.reshape(b, s, H, dk, M)
            return jnp.transpose(y, (0, 2, 1, 3, 4))
        qh = proj(q, Wq, bq)
        kh = proj(k, Wk, bk)
        vh = proj(v, Wv, bv)

        def interfere(x):
            return x + 0.1 * amp[0] * jnp.einsum('bhsdi,hij->bhsdj', x, interference)
        qh, kh, vh = (interfere(qh), interfere(kh), interfere(vh))
        scores = jnp.einsum('bhqdm,bhkdm->bhqkm', qh, kh) / math.sqrt(dk)
        weights = jax.nn.softmax(scores, axis=3)
        out = jnp.einsum('bhqkm,bhkdm->bhqdm', weights, vh)
        out = jnp.transpose(out, (0, 2, 1, 3, 4)).reshape(b, s, dm)
        return out @ Wo.T + bo

    def _L0_ffn_ref(x, gate_wq, gate_scale, up_wq, up_scale, down_wq, down_scale):
        import jax, jax.numpy as jnp
        import numpy as np

        def _dequant_linear(x, wq, scale):
            w = wq.astype(jnp.float32) * scale[:, None]
            return jnp.einsum('bsh,oh->bso', x, w)
        gate = _dequant_linear(x, gate_wq, gate_scale)
        up = _dequant_linear(x, up_wq, up_scale)
        h = jax.nn.silu(gate) * up
        return _dequant_linear(h, down_wq, down_scale)
    x = x + _L0_xattn_ref(_layernorm(x, axis=-1), ctx_4096, ctx_4096, L0_xattn_Wq, L0_xattn_bq, L0_xattn_Wk, L0_xattn_bk, L0_xattn_Wv, L0_xattn_bv, L0_xattn_interference, L0_xattn_amp, L0_xattn_Wo, L0_xattn_bo)
    x = x + _L0_ffn_ref(_layernorm(x, axis=-1), L0_ffn_gate_wq, L0_ffn_gate_scale, L0_ffn_up_wq, L0_ffn_up_scale, L0_ffn_down_wq, L0_ffn_down_scale)
    return x

_drawn_inputs = setup_inputs


def setup_inputs(seed=0):
    import zlib

    import numpy as np

    out = dict(_drawn_inputs(seed))
    spreads = {'L0_xattn_bq': (0.0, 0.8),
     'L0_xattn_bk': (0.0, 0.8),
     'L0_xattn_bv': (0.0, 0.1),
     'L0_xattn_bo': (0.0, 0.1)}
    factors = {}
    for name, (base, spread) in spreads.items():
        noise = np.random.default_rng([zlib.crc32(name.encode()), seed]).standard_normal(out[name].shape)
        drawn = base * np.exp(spread * noise) if base else spread * noise
        out[name] = jnp.asarray(drawn.astype(out[name].dtype))
    for name, factor in factors.items():
        out[name] = (out[name] * factor).astype(out[name].dtype)
    return out
```

```python
from contextlib import ExitStack

import concourse.bass as bass
from concourse import mybir

F32 = mybir.dt.float32
F32R = mybir.dt.float32r
F16 = mybir.dt.float16
BF16 = mybir.dt.bfloat16
I32 = mybir.dt.int32
ALU = mybir.AluOpType
ACT = mybir.ActivationFunctionType
AX = mybir.AxisListType.X

P = 128
NB = 16
D = 1024
KT = D // P
HEADS, STATES, DK = 16, 4, 16
PAIRS = P // DK
HT = P // (STATES * DK)
VP = 3 * DK + 1
VS = VP + 1
STEPS = NB * KT
SCALE = DK ** -0.5
E_SHIFT = 9.704060527839234
EPS = 1e-5
HID = 3584
FT = HID // P
FB = 2
NBLK = FT // FB
CH = 512
NCH = NB * P // CH
TPC = CH // P
XS = 256.0


def until(eng, sem, value):
    if not isinstance(value, int) or value > 0:
        eng.wait_ge(sem, value)


def apart(eng, passed):
    eng.sem_inc(passed, 1)


def program(nc, x, ctx_t, wqkv, b_qk, b_v, mix_rows, amp, wo_t, b_o, gate_w, gate_s, up_w, up_s,
            down_w, down_s, ident_c, pair_mask_c, fold_mask_c, state_eye_c, out):
    ot_scratch = nc.dram_tensor("ot_scratch", (NB, P, KT, P), F32, kind="Internal").ap()
    x1_scratch = nc.dram_tensor("x1_scratch", (NB, P, D), F32, kind="Internal").ap()

    with ExitStack() as ctx:
        def sb(name, shape, dt, scope=ctx):
            return scope.enter_context(nc.sbuf_tensor(name, shape, dt))

        def sem(name):
            return ctx.enter_context(nc.semaphore(name))

        banks = [ctx.enter_context(nc.psum_tensor(f"banks{i}", [P, 2, 512], F32)) for i in range(4)]

        ident = sb("ident", [P, P], F32)
        pair_mask = sb("pair_mask", [P, PAIRS], F32)

        b_scope = ExitStack()
        W = sb("W", [P, 3, KT, D], F32, b_scope)
        bias_qk = sb("bias_qk", [P, KT, 2], F32, b_scope)
        bias_v = sb("bias_v", [P, D], F32, b_scope)
        xin = sb("xin", [P, 2, D], F32, b_scope)
        xn = sb("xn", [P, 2, D], F32, b_scope)
        xn_t = sb("xn_t", [P, 2, KT, P], F32, b_scope)
        ctxt = sb("ctxt", [P, 2, KT, P], F32, b_scope)
        stats = sb("stats", [P, 2, 6], F32, b_scope)
        moments = sb("moments", [P, 2], F32, b_scope)
        var_eps = sb("var_eps", [P, 1], F32, b_scope)
        minus_half = sb("minus_half", [P, 1], F32, b_scope)
        rstd = sb("rstd", [P, 1], F32, b_scope)
        a_scope = ExitStack()
        w_raw = sb("w_raw", [P, 4, D], F32, a_scope)
        fold = sb("fold", [P, KT, P], F32, a_scope)
        fold_mask = sb("fold_mask", [P, HT, DK], F32, a_scope)
        state_eye = sb("state_eye", [P, STATES], F32, a_scope)
        mix = sb("mix", [P, KT, STATES], F32, a_scope)
        amp_sb = sb("amp_sb", [P, 1], F32, a_scope)
        amp_tenth = sb("amp_tenth", [P, 1], F32, a_scope)
        bqk_raw = sb("bqk_raw", [P, KT, 2], F32, a_scope)
        bv_raw = sb("bv_raw", [P, KT], F32, a_scope)
        bv_wide = sb("bv_wide", [P, KT, P], F32, a_scope)
        a_scope.close()
        q_t = sb("q_t", [P, 2, P], F32, b_scope)
        k_wide = sb("k_wide", [P, 2, PAIRS, P], F32, b_scope)
        v_f = sb("v_f", [P, 2, P], F32, b_scope)
        v_rest = sb("v_rest", [P, 2, P], F32, b_scope)
        v_parts = sb("v_parts", [P, 4, PAIRS, VS], BF16, b_scope)
        neg_max = sb("neg_max", [P, 2, PAIRS], F32, b_scope)
        s_m = sb("s_m", [P, 2, PAIRS, P], F32, b_scope)
        e_f = sb("e_f", [P, 2, PAIRS, P], F32, b_scope)
        e_hi = sb("e_hi", [P, 2, PAIRS, P], F16, b_scope)
        e_lo = sb("e_lo", [P, 2, PAIRS, P], F16, b_scope)
        o_sum = sb("o_sum", [P, 2, PAIRS, DK], F32, b_scope)
        r_den = sb("r_den", [P, 2, PAIRS, 1], F32, b_scope)
        o_tok = sb("o_tok", [P, 2, P], F32, b_scope)
        o_t = sb("o_t", [P, 2, P], F32, b_scope)
        b_scope.close()

        xh = sb("xh", [P, KT, NB * P], F16)
        xl = sb("xl", [P, KT, NB * P], F16)
        c_scope = ExitStack()
        wo_raw = sb("wo_raw", [P, 2, D], F32, c_scope)
        wo_hi = sb("wo_hi", [P, KT, D], F32R, c_scope)
        wo_lo = sb("wo_lo", [P, KT, D], F32R, c_scope)
        bo_rows = sb("bo_rows", [P, D], F32, c_scope)
        ot_in = sb("ot_in", [P, 2, D], F32, c_scope)
        ot_hi = sb("ot_hi", [P, 2, D], F32R, c_scope)
        ot_lo = sb("ot_lo", [P, 2, D], F32R, c_scope)
        x_again = sb("x_again", [P, 2, D], F32, c_scope)
        x1 = sb("x1", [P, 2, D], F32, c_scope)
        xn2 = sb("xn2", [P, 1, D], F32, c_scope)
        c_stats = sb("c_stats", [P, 2, 6], F32, c_scope)
        c_moments = sb("c_moments", [P, 2], F32, c_scope)
        c_var = sb("c_var", [P, 1], F32, c_scope)
        c_pow = sb("c_pow", [P, 1], F32, c_scope)
        c_half = sb("c_half", [P, 1], F32, c_scope)
        c_rstd = sb("c_rstd", [P, 1], F32, c_scope)
        c_scope.close()

        d_scope = ExitStack()
        acc = sb("acc", [P, NB, D], F32, d_scope)
        gu_raw = sb("gu_raw", [P, 2, D], I32, d_scope)
        d_raw = sb("d_raw", [P, 2, D], I32, d_scope)
        gu_w = sb("gu_w", [P, 2, 2, FB, KT, P], F16, d_scope)
        d_w = sb("d_w", [P, 2, FB, D], F32R, d_scope)
        silu = sb("silu", [P, 2, CH], F32, d_scope)
        h_f = sb("h_f", [P, 2, CH], F32, d_scope)
        h_hi = sb("h_hi", [P, 2, FB, CH], F32R, d_scope)
        h_lo = sb("h_lo", [P, 2, FB, CH], F32R, d_scope)
        g_s = sb("g_s", [P, FT], F32, d_scope)
        u_s = sb("u_s", [P, FT], F32, d_scope)
        g_sx = sb("g_sx", [P, FT], F32, d_scope)
        u_sx = sb("u_sx", [P, FT], F32, d_scope)
        ds_rows = sb("ds_rows", [P, D], F32, d_scope)
        x1_in = gu_raw[:].bitcast(F32)
        d_scope.close()

        act_passed, dve_passed, pool_passed = sem("act_passed"), sem("dve_passed"), sem("pool_passed")
        const_loaded = sem("const_loaded")
        w_loaded = [sem(f"w_loaded{i}") for i in range(4)]
        amp_ready, mix_ready, fold_ready = sem("amp_ready"), sem("mix_ready"), sem("fold_ready")
        bv_wide_ready = sem("bv_wide_ready")
        bias_made, bias_ready = sem("bias_made"), sem("bias_ready")
        w_folded, w_even_free, w_odd_free = sem("w_folded"), sem("w_even_free"), sem("w_odd_free")
        x_loaded = [sem("x_loaded0"), sem("x_loaded1")]
        ctx_loaded = [sem("ctx_loaded0"), sem("ctx_loaded1")]
        half_ready = sem("half_ready")
        stats_ready, moments_ready = sem("stats_ready"), sem("moments_ready")
        var_ready, rstd_ready, xn_ready = sem("var_ready"), sem("rstd_ready"), sem("xn_ready")
        xn_transposed, xn_t_kept = sem("xn_transposed"), sem("xn_t_kept")
        projected = sem("projected")
        q_kept, k_kept, v_kept = sem("q_kept"), sem("k_kept"), sem("v_kept")
        ones_ready, v_chain, v_split = sem("ones_ready"), sem("v_chain"), sem("v_split")
        scored, max_ready, sm_ready = sem("scored"), sem("max_ready"), sem("sm_ready")
        s_transposed, e_hi_ready, e_ready = sem("s_transposed"), sem("e_hi_ready"), sem("e_ready")
        e_lo_ready, attended = sem("e_lo_ready"), sem("attended")
        o_summed, den_ready, o_ready = sem("o_summed"), sem("den_ready"), sem("o_ready")
        o_transposed, o_t_kept = sem("o_transposed"), sem("o_t_kept")
        o_t_stored = [sem("o_t_stored0"), sem("o_t_stored1")]

        bo_loaded, wo_loaded = sem("bo_loaded"), [sem("wo_loaded0"), sem("wo_loaded1")]
        wo_hi_ready, wo_lo_ready = sem("wo_hi_ready"), sem("wo_lo_ready")
        ot_loaded, xa_loaded = [sem("ot_loaded0"), sem("ot_loaded1")], [sem("xa_loaded0"), sem("xa_loaded1")]
        ot_hi_ready, ot_lo_ready, xb_ready = sem("ot_hi_ready"), sem("ot_lo_ready"), sem("xb_ready")
        o_projected, x1_ready = sem("o_projected"), sem("x1_ready")
        x1_stored = [sem("x1_stored0"), sem("x1_stored1")]
        c_half_ready, c_stats_ready, c_moments_ready = sem("c_half_ready"), sem("c_stats_ready"), sem("c_moments_ready")
        c_var_ready, c_rstd_ready, xn2_ready = sem("c_var_ready"), sem("c_rstd_ready"), sem("xn2_ready")
        xn2_transposed, xh_ready, xl_ready = sem("xn2_transposed"), sem("xh_ready"), sem("xl_ready")
        scales_loaded, scales_ready = sem("scales_loaded"), sem("scales_ready")
        gu_loaded, d_loaded = [sem("gu_loaded0"), sem("gu_loaded1")], [sem("d_loaded0"), sem("d_loaded1")]
        gu_ready, d_ready = sem("gu_ready"), sem("d_ready")
        gated, upped, silu_ready = sem("gated"), sem("upped"), sem("silu_ready")
        h_ready, h_hi_ready, h_lo_ready = sem("h_ready"), sem("h_hi_ready"), sem("h_lo_ready")
        downed, acc_added, acc_scaled = sem("downed"), sem("acc_added"), sem("acc_scaled")
        x1_loaded, y_ready, y_stored = [sem("x1_loaded0"), sem("x1_loaded1")], sem("y_ready"), sem("y_stored")

        S_ps, T_ps, QKV_ps = banks[0], banks[1], banks[2]
        PV_ps = banks[3][:, 0, :]
        XT_ps = banks[3][:, 1, 0:P]
        OT_ps = banks[3][:, 1, P:2 * P]
        S_flat = S_ps[:].rearrange("p b n -> p (b n)")
        T_flat = T_ps[:].rearrange("p b n -> p (b n)")
        S_pairs = S_flat.rearrange("p (c k) -> p c k", c=PAIRS)
        T_pairs = T_flat.rearrange("p (c k) -> p c k", c=PAIRS)
        PV_pairs = PV_ps[:, 0:PAIRS * VP].rearrange("p (c n) -> p c n", n=VP)

        ab_scope = ExitStack()
        block = ab_scope.enter_context(nc.Block())

        @block.sync
        def _(sp):
            small = [(ident[:], ident_c), (pair_mask[:], pair_mask_c), (fold_mask[:], fold_mask_c),
                     (state_eye[:], state_eye_c), (mix[:], mix_rows), (bqk_raw[:], b_qk), (bv_raw[:], b_v),
                     (amp_sb[:], amp.partition_broadcast(P))]
            for dst, src in small:
                sp.dma_start(dst, src).then_inc(const_loaded, 16)
            sp.dma_start(xin[:, 0], x[0]).then_inc(x_loaded[0], 16)
            sp.dma_start(xin[:, 1], x[1]).then_inc(x_loaded[1], 16)
            sp.dma_start(ctxt[:, 0], ctx_t[0]).then_inc(ctx_loaded[0], 16)
            for j in range(4):
                sp.dma_start(w_raw[:, j], wqkv[j]).then_inc(w_loaded[j], 16)
            with sp.Fori(1, 3 * KT // 4) as g:
                for j in range(4):
                    sp.wait_ge(w_folded, 4 * g + j - 3)
                    sp.dma_start(w_raw[:, j], wqkv[4 * g + j]).then_inc(w_loaded[j], 16)

            def steps(base, batch, ts):
                for t in ts:
                    b, j = batch + t // KT, t % KT
                    if j == 0:
                        if not (isinstance(b, int) and b + 2 >= NB):
                            sp.wait_ge(xn_ready, b + 1)
                            sp.dma_start(xin[:, t // KT], x[b + 2]).then_inc(x_loaded[t // KT], 16)
                        if not (isinstance(b, int) and b + 1 >= NB):
                            until(sp, projected, KT * b)
                            n = (t // KT + 1) % 2
                            sp.dma_start(ctxt[:, n], ctx_t[b + 1]).then_inc(ctx_loaded[n], 16)
                    r, w = base + t - 5, (t - 5) % 2
                    if isinstance(r, int) and r < 0:
                        continue
                    rb, rj = batch + (t - 5) // KT, (t - 5) % KT
                    sp.wait_ge(o_t_kept, r + 1)
                    sp.dma_start(ot_scratch[rb, :, rj, :], o_t[:, w]).then_inc(o_t_stored[w], 16)

            steps(0, 0, range(16))
            with sp.Fori(1, NB // 2 - 1) as i:
                steps(i * 16, i * 2, range(16))
            steps(STEPS - 16, NB - 2, range(16))
            steps(STEPS - 16, NB - 2, range(16, 21))
            for q in o_t_stored:
                sp.wait_ge(q, 16 * STEPS // 2)

        @block.gpsimd
        def _(pool):
            pool.memset(minus_half[:], -0.5).then_inc(half_ready, 1)
            pool.wait_ge(half_ready, 1)

            def root(n):
                pool.wait_ge(var_ready, n + 1)
                pool.tensor_tensor(rstd[:], var_eps[:], minus_half[:], ALU.pow).then_inc(rstd_ready, 1)

            root(0)
            root(1)
            pool.wait_ge(w_folded, 3 * KT)
            pool.wait_ge(bias_made, 1)
            pool.memset(v_parts[:, :, :, VP - 1:VP], 1.0).then_inc(ones_ready, 1)

            def steps(base, batch, ts):
                for t in ts:
                    s, b, j = base + t, batch + t // KT, t % KT
                    if t < 16:
                        pool.wait_ge(v_kept, s + 1)
                        until(pool, attended, s - 3)
                        part = [v_parts[:, t % 4, :, DK * q:DK * (q + 1)] for q in range(3)]
                        whole = v_f[:, t % 2].rearrange("p (c d) -> p c d", d=DK)
                        apart(pool, pool_passed)
                        rest = v_rest[:, t % 2].rearrange("p (c d) -> p c d", d=DK)
                        pool.tensor_copy(part[0], whole).then_inc(v_chain, 1)
                        pool.wait_ge(v_chain, 3 * s + 1)
                        pool.tensor_tensor(rest, whole, part[0], ALU.subtract).then_inc(v_chain, 1)
                        pool.wait_ge(v_chain, 3 * s + 2)
                        apart(pool, pool_passed)
                        pool.tensor_copy(part[1], rest).then_inc(v_chain, 1)
                        pool.wait_ge(v_chain, 3 * s + 3)
                        pool.tensor_tensor(part[2], rest, part[1], ALU.subtract).then_inc(v_split, 1)
                    r = s - 2
                    if not (isinstance(r, int) and r < 0) and t < 18:
                        pool.wait_ge(e_ready, r + 1)
                        pool.wait_ge(e_hi_ready, r + 1)
                        until(pool, attended, r - 1)
                        pool.tensor_tensor(e_lo[:, t % 2], e_f[:, t % 2], e_hi[:, t % 2],
                                           ALU.subtract).then_inc(e_lo_ready, 1)
                    if j == 5 and t < 16 and not (isinstance(b, int) and b + 2 >= NB):
                        root(b + 2)

            steps(0, 0, range(16))
            with pool.Fori(1, NB // 2 - 1) as i:
                steps(i * 16, i * 2, range(16))
            steps(STEPS - 16, NB - 2, range(18))

        @block.scalar
        def _(act):
            act.sem_inc(w_even_free, 1)
            with act.Fori(0, 3) as m:
                for j in range(0, KT, 2):
                    act.wait_ge(w_folded, 8 * m + j + 1)
                    apart(act, act_passed)
                    act.activation(W[:, m, :, j * P:(j + 1) * P], S_pairs, ACT.Copy).then_inc(w_even_free, 1)

            def keep_xn_t(n, slot, j, before):
                act.wait_ge(xn_transposed, n + 1)
                if j == 0:
                    until(act, projected, before)
                act.activation(xn_t[:, slot, j], XT_ps, ACT.Copy).then_inc(xn_t_kept, 1)

            for j in range(KT):
                keep_xn_t(j, 0, j, 0)
            act.wait_ge(bias_ready, 2)

            def steps(base, batch, ts):
                for t in ts:
                    s, b, j = base + t, batch + t // KT, t % KT
                    r = s - 5
                    if not (isinstance(r, int) and r < 0):
                        w = (t - 5) % 2
                        act.wait_ge(o_transposed, r + 1)
                        until(act, o_t_stored[w], 8 * (r - w))
                        act.activation(o_t[:, w], OT_ps, ACT.Copy).then_inc(o_t_kept, 1)
                    if t < 16:
                        act.wait_ge(projected, s + 1)
                        until(act, scored, s - 1)
                        act.activation(q_t[:, t % 2], QKV_ps[:, t % 2, 0:P], ACT.Identity,
                                       bias=bias_qk[:, j, 0:1]).then_inc(q_kept, 1)
                        if not (isinstance(b, int) and b + 1 >= NB):
                            keep_xn_t(s + KT, (t // KT + 1) % 2, j, KT * b)
                    r = s - 2
                    if not (isinstance(r, int) and r < 0) and t < 18:
                        act.wait_ge(s_transposed, r + 1)
                        until(act, attended, r - 1)
                        act.activation(e_hi[:, t % 2], T_pairs, ACT.Exp, bias=E_SHIFT, scale=SCALE)\
                           .then_inc(e_hi_ready, 1)
                        until(act, e_lo_ready, r - 1)
                        act.activation(e_f[:, t % 2], T_pairs, ACT.Exp, bias=E_SHIFT, scale=SCALE)\
                           .then_inc(e_ready, 1)

            steps(0, 0, range(16))
            with act.Fori(1, NB // 2 - 1) as i:
                steps(i * 16, i * 2, range(16))
            steps(STEPS - 16, NB - 2, range(21))

        @block.vector
        def _(dve):
            dve.wait_ge(const_loaded, 16 * 8)
            dve.tensor_scalar(amp_tenth[:], amp_sb[:], 0.1, None, ALU.mult).then_inc(amp_ready, 1)
            dve.wait_ge(amp_ready, 1)
            dve.scalar_tensor_tensor(out=mix[:], in0=mix[:], scalar=amp_tenth[:, 0:1],
                                     in1=state_eye[:].unsqueeze(1).to_broadcast([P, KT, STATES]),
                                     op0=ALU.mult, op1=ALU.add).then_inc(mix_ready, 1)
            dve.wait_ge(mix_ready, 1)
            for j in range(KT):
                for h in range(HT):
                    width = STATES * DK
                    dve.tensor_tensor(
                        fold[:, j, h * width:(h + 1) * width].rearrange("p (m d) -> p m d", d=DK),
                        mix[:, j].unsqueeze(2).to_broadcast([P, STATES, DK]),
                        fold_mask[:, h:h + 1, :].to_broadcast([P, STATES, DK]), ALU.mult).then_inc(fold_ready, 1)
            dve.tensor_tensor(bv_wide[:], bv_raw[:].unsqueeze(2).to_broadcast([P, KT, P]),
                              ident[:, 0:1].unsqueeze(1).to_broadcast([P, KT, P]), ALU.bypass)\
               .then_inc(bv_wide_ready, 1)

            def moments_of(n, slot):
                if isinstance(n, int):
                    dve.wait_ge(x_loaded[slot], 16 * (n // 2 + 1))
                else:
                    dve.wait_ge(x_loaded[slot], 8 * (n - slot + 2))
                for q in range(2):
                    dve.bn_stats(stats[:, q], xin[:, slot, q * 512:(q + 1) * 512]).then_inc(stats_ready, 1)
                dve.wait_ge(stats_ready, 2 * n + 2)
                apart(dve, dve_passed)
                dve.bn_aggr(moments[:], stats[:].rearrange("p a b -> p (a b)")).then_inc(moments_ready, 1)
                dve.wait_ge(moments_ready, n + 1)
                until(dve, rstd_ready, n)
                dve.tensor_scalar(var_eps[:], moments[:, 1:2], EPS, None, ALU.add).then_inc(var_ready, 1)

            def normalise(n, slot, before):
                dve.wait_ge(rstd_ready, n + 1)
                until(dve, xn_transposed, before)
                dve.tensor_scalar(xn[:, slot], xin[:, slot], moments[:, 0:1], rstd[:, 0:1],
                                  ALU.subtract, ALU.mult).then_inc(xn_ready, 1)

            for n in range(2):
                moments_of(n, n)
                normalise(n, n, 0)
                until(dve, xn_ready, n + 1)

            dve.sem_inc(w_odd_free, 1)
            with dve.Fori(0, 3) as m:
                for j in range(1, KT, 2):
                    dve.wait_ge(w_folded, 8 * m + j + 1)
                    dve.tensor_copy(W[:, m, :, j * P:(j + 1) * P], T_pairs).then_inc(w_odd_free, 1)
            dve.wait_ge(bias_made, 1)
            dve.tensor_copy(bias_qk[:], QKV_ps[:, 0, 0:2 * KT].rearrange("p (j m) -> p j m", m=2))\
               .then_inc(bias_ready, 1)
            dve.tensor_copy(bias_v[:], banks[3][:].rearrange("p b n -> p (b n)")).then_inc(bias_ready, 1)
            dve.wait_ge(bias_ready, 2)

            def steps(base, batch, ts):
                for t in ts:
                    s, b, j = base + t, batch + t // KT, t % KT
                    if t < 16:
                        dve.wait_ge(q_kept, s + 1)
                        until(dve, scored, s - 1)
                        dve.scalar_tensor_tensor(
                            out=k_wide[:, t % 2],
                            in0=QKV_ps[:, t % 2, P:2 * P].unsqueeze(1).to_broadcast([P, PAIRS, P]),
                            scalar=bias_qk[:, j, 1:2],
                            in1=pair_mask[:].unsqueeze(2).to_broadcast([P, PAIRS, P]),
                            op0=ALU.add, op1=ALU.mult).then_inc(k_kept, 1)
                        until(dve, v_split, s - 1)
                        dve.tensor_tensor(v_f[:, t % 2], QKV_ps[:, t % 2, 2 * P:3 * P],
                                          bias_v[:, j * P:(j + 1) * P], ALU.add).then_inc(v_kept, 1)
                    r = s - 1
                    if not (isinstance(r, int) and r < 0) and t < 17:
                        dve.wait_ge(scored, r + 1)
                        until(dve, sm_ready, r - 1)
                        dve.tensor_reduce(neg_max[:, (t - 1) % 2], S_pairs, AX, ALU.max, negate=True)\
                           .then_inc(max_ready, 1)
                        dve.wait_ge(max_ready, r + 1)
                        until(dve, s_transposed, r - 1)
                        dve.tensor_tensor(s_m[:, (t - 1) % 2], S_pairs,
                                          neg_max[:, (t - 1) % 2].unsqueeze(2).to_broadcast([P, PAIRS, P]),
                                          ALU.add).then_inc(sm_ready, 1)
                    r = s - 3
                    if not (isinstance(r, int) and r < 0) and t < 19:
                        w = (t - 3) % 2
                        dve.wait_ge(attended, r + 1)
                        until(dve, o_ready, r - 1)
                        dve.tensor_reduce(o_sum[:, w], PV_pairs[:, :, 0:3 * DK].rearrange("p c (q d) -> p c d q", q=3),
                                          AX, ALU.add).then_inc(o_summed, 1)
                        dve.reciprocal(r_den[:, w], PV_pairs[:, :, VP - 1:VP]).then_inc(den_ready, 1)
                        dve.wait_ge(o_summed, r + 1)
                        dve.wait_ge(den_ready, r + 1)
                        until(dve, o_transposed, r - 1)
                        dve.tensor_tensor(o_tok[:, w].rearrange("p (c d) -> p c d", d=DK), o_sum[:, w],
                                          r_den[:, w].to_broadcast([P, PAIRS, DK]), ALU.mult).then_inc(o_ready, 1)
                    if t < 16 and not (isinstance(b, int) and b + 2 >= NB):
                        if j == 4:
                            moments_of(b + 2, t // KT)
                        if j == 6:
                            normalise(b + 2, t // KT, KT * (b + 1))

            steps(0, 0, range(16))
            with dve.Fori(1, NB // 2 - 1) as i:
                steps(i * 16, i * 2, range(16))
            steps(STEPS - 16, NB - 2, range(19))

        @block.tensor
        def _(pe):
            pe.wait_ge(const_loaded, 16 * 8)
            pe.wait_ge(fold_ready, KT * HT)
            with pe.Fori(0, 3) as m:
                for j in range(KT):
                    pe.wait_ge(w_loaded[j % 4], 32 * m + 16 * (j // 4) + 16)
                    if j % 2 == 0:
                        pe.wait_ge(w_even_free, 4 * m + j // 2 + 1)
                    else:
                        pe.wait_ge(w_odd_free, 4 * m + j // 2 + 1)
                    for k in range(KT):
                        mm = pe.matmul((S_pairs, T_pairs)[j % 2][:, k, :], w_raw[:, j % 4, k * P:(k + 1) * P],
                                       fold[:, j, :], start=True, stop=True)
                    mm.then_inc(w_folded, 1)
            pe.wait_ge(bv_wide_ready, 1)
            for j in range(KT):
                pe.matmul(QKV_ps[:, 0, 2 * j:2 * j + 2], fold[:, j, :], bqk_raw[:, j, :], start=True, stop=True)
            for j in range(KT):
                mm = pe.matmul(banks[3][:, j // 4, (j % 4) * P:(j % 4 + 1) * P], bv_wide[:, j, :], fold[:, j, :],
                               start=True, stop=True)
            mm.then_inc(bias_made, 1)

            def transpose_xn(n, slot, j):
                until(pe, xn_t_kept, n)
                until(pe, o_t_kept, n - KT - 4)
                pe.transpose(XT_ps, xn[:, slot, j * P:(j + 1) * P], ident[:]).then_inc(xn_transposed, 1)

            pe.wait_ge(xn_ready, 1)
            pe.wait_ge(bias_ready, 2)
            for j in range(KT):
                transpose_xn(j, 0, j)

            def steps(base, batch, ts):
                for t in ts:
                    s, b, j = base + t, batch + t // KT, t % KT
                    here = t // KT % 2
                    r = s - 5
                    if not (isinstance(r, int) and r < 0):
                        pe.wait_ge(o_ready, r + 1)
                        until(pe, o_t_kept, r)
                        if not (isinstance(r, int) and s + KT > STEPS):
                            pe.wait_ge(xn_t_kept, s + KT)
                        pe.transpose(OT_ps, o_tok[:, (t - 5) % 2], ident[:]).then_inc(o_transposed, 1)
                    if t < 16:
                        if j == 0:
                            pe.wait_ge(xn_t_kept, KT * (b + 1))
                            if isinstance(b, int):
                                pe.wait_ge(ctx_loaded[here], 16 * (b // 2 + 1))
                            else:
                                pe.wait_ge(ctx_loaded[here], 8 * (b - here + 2))
                        cols = slice(j * P, (j + 1) * P)
                        until(pe, v_kept, s - 1)
                        for k in range(KT):
                            mm = pe.matmul(QKV_ps[:, t % 2, 0:P], W[:, 0, k, cols], xn_t[:, here, k],
                                           start=(k == 0), stop=(k == KT - 1))
                        for k in range(KT):
                            mm = pe.matmul(QKV_ps[:, t % 2, P:2 * P], W[:, 1, k, cols], ctxt[:, here, k],
                                           start=(k == 0), stop=(k == KT - 1))
                        for k in range(KT):
                            mm = pe.matmul(QKV_ps[:, t % 2, 2 * P:3 * P], ctxt[:, here, k], W[:, 2, k, cols],
                                           start=(k == 0), stop=(k == KT - 1))
                        mm.then_inc(projected, 1)
                        if not (isinstance(b, int) and b + 1 >= NB):
                            if j == 0:
                                pe.wait_ge(xn_ready, b + 2)
                            transpose_xn(s + KT, 1 - here, j)
                    r = s - 1
                    if not (isinstance(r, int) and r < 0) and t < 17:
                        pe.wait_ge(q_kept, r + 1)
                        pe.wait_ge(k_kept, r + 1)
                        until(pe, sm_ready, r)
                        for h in range(2):
                            mm = pe.matmul(S_ps[:, h], q_t[:, (t - 1) % 2],
                                           k_wide[:, (t - 1) % 2, 4 * h:4 * h + 4].rearrange("p c k -> p (c k)"),
                                           start=True, stop=True)
                        mm.then_inc(scored, 1)
                    r = s - 2
                    if not (isinstance(r, int) and r < 0) and t < 18:
                        pe.wait_ge(sm_ready, r + 1)
                        until(pe, e_ready, r)
                        for c in range(PAIRS):
                            mm = pe.transpose(T_pairs[:, c, :], s_m[:, t % 2, c, :], ident[:])
                        mm.then_inc(s_transposed, 1)
                    r = s - 3
                    if not (isinstance(r, int) and r < 0) and t < 19:
                        pe.wait_ge(e_hi_ready, r + 1)
                        pe.wait_ge(e_lo_ready, r + 1)
                        pe.wait_ge(v_split, r + 1)
                        if isinstance(r, int) and r == 0:
                            pe.wait_ge(ones_ready, 1)
                        until(pe, o_summed, r)
                        until(pe, den_ready, r)
                        for c in range(PAIRS):
                            for e in (e_hi, e_lo):
                                mm = pe.matmul(PV_pairs[:, c, :], e[:, (t - 3) % 2, c, :],
                                               v_parts[:, (t - 3) % 4, c, 0:VP], start=(e is e_hi), stop=(e is e_lo))
                        mm.then_inc(attended, 1)

            steps(0, 0, range(16))
            with pe.Fori(1, NB // 2 - 1) as i:
                steps(i * 16, i * 2, range(16))
            steps(STEPS - 16, NB - 2, range(21))

        ab_scope.close()

        c_block = ExitStack()
        block = c_block.enter_context(nc.Block())
        O_ps = [b[:].rearrange("p b n -> p (b n)") for b in banks[0:2]]
        X2_ps = banks[2][:].rearrange("p b (k t) -> p (b k) t", t=P)
        xh_b = xh[:].rearrange("p k (b t) -> p k b t", t=P)
        xl_b = xl[:].rearrange("p k (b t) -> p k b t", t=P)
        real = lambda r: not (isinstance(r, int) and r < 0)

        def pairs_of_batches(eng, steps, tail):
            steps(0, range(2))
            with eng.Fori(1, NB // 2) as i:
                steps(i * 2, range(2))
            steps(NB - 2, range(2, 2 + tail))

        @block.sync
        def _(sp):
            sp.dma_start(bo_rows[:], b_o.partition_broadcast(P)).then_inc(bo_loaded, 16)
            for j in range(2):
                sp.dma_start(wo_raw[:, j], wo_t[j]).then_inc(wo_loaded[j], 16)
            for j in range(2, KT):
                sp.wait_ge(wo_lo_ready, j - 1)
                sp.dma_start(wo_raw[:, j % 2], wo_t[j]).then_inc(wo_loaded[j % 2], 16)

            def steps(base, ts):
                for t in ts:
                    b, q = base + t, t % 2
                    if t < 2:
                        until(sp, ot_lo_ready, b - 1)
                        sp.dma_start(ot_in[:, q], ot_scratch[b].rearrange("p k t -> p (k t)")).then_inc(ot_loaded[q], 16)
                        until(sp, x1_ready, b - 1)
                        sp.dma_start(x_again[:, q], x[b]).then_inc(xa_loaded[q], 16)
                    if real(b - 2):
                        sp.wait_ge(x1_ready, b - 1)
                        sp.dma_start(x1_scratch[b - 2], x1[:, q]).then_inc(x1_stored[q], 16)

            pairs_of_batches(sp, steps, 2)
            for q in range(2):
                sp.wait_ge(x1_stored[q], 16 * NB // 2)

        @block.gpsimd
        def _(pool):
            pool.memset(c_half[:], -0.5).then_inc(c_half_ready, 1)
            pool.wait_ge(c_half_ready, 1)
            pool.wait_ge(bo_loaded, 16)

            def steps(base, ts):
                for t in ts:
                    b, q = base + t, t % 2
                    if t < 2:
                        pool.wait_ge(xa_loaded[q], 8 * (b - q) + 16)
                        pool.tensor_tensor(x_again[:, q], x_again[:, q], bo_rows[:], ALU.add).then_inc(xb_ready, 1)
                    if real(b - 1):
                        pool.wait_ge(c_var_ready, b)
                        pool.tensor_tensor(c_rstd[:], c_var[:], c_half[:], ALU.pow).then_inc(c_rstd_ready, 1)

            pairs_of_batches(pool, steps, 1)

        @block.scalar
        def _(act):
            for j in range(KT):
                act.wait_ge(wo_loaded[j % 2], 16 * (j // 2 + 1))
                act.activation(wo_hi[:, j], wo_raw[:, j % 2], ACT.Copy).then_inc(wo_hi_ready, 1)

            def steps(base, ts):
                for t in ts:
                    b, q = base + t, t % 2
                    if t < 2:
                        act.wait_ge(ot_loaded[q], 8 * (b - q) + 16)
                        until(act, o_projected, b - 1)
                        act.activation(ot_hi[:, q], ot_in[:, q], ACT.Copy).then_inc(ot_hi_ready, 1)
                    if real(b - 2):
                        act.wait_ge(xn2_transposed, b - 1)
                        apart(act, act_passed)
                        act.activation(xh_b[:, :, b - 2, :], X2_ps, ACT.Copy).then_inc(xh_ready, 1)

            pairs_of_batches(act, steps, 2)

        @block.vector
        def _(dve):
            for j in range(KT):
                dve.wait_ge(wo_hi_ready, j + 1)
                dve.tensor_tensor(wo_lo[:, j], wo_raw[:, j % 2], wo_hi[:, j].bitcast(F32), ALU.subtract)\
                   .then_inc(wo_lo_ready, 1)

            def steps(base, ts):
                for t in ts:
                    b, q = base + t, t % 2
                    if t < 2:
                        dve.wait_ge(ot_hi_ready, b + 1)
                        until(dve, o_projected, b - 1)
                        dve.tensor_tensor(ot_lo[:, q], ot_in[:, q], ot_hi[:, q].bitcast(F32), ALU.subtract)\
                           .then_inc(ot_lo_ready, 1)
                    if real(b - 2):
                        dve.wait_ge(xh_ready, b - 1)
                        dve.tensor_tensor(xl_b[:, :, b - 2, :], X2_ps, xh_b[:, :, b - 2, :], ALU.subtract)\
                           .then_inc(xl_ready, 1)
                    if real(b - 1) and t < 3:
                        r, w = b - 1, (t - 1) % 2
                        dve.wait_ge(o_projected, r + 1)
                        dve.wait_ge(xb_ready, r + 1)
                        until(dve, x1_stored[w], 8 * (r - w))
                        dve.tensor_tensor(x1[:, w], O_ps[w], x_again[:, w], ALU.add).then_inc(x1_ready, 1)
                        dve.wait_ge(x1_ready, r + 1)
                        for h in range(2):
                            dve.bn_stats(c_stats[:, h], x1[:, w, h * 512:(h + 1) * 512]).then_inc(c_stats_ready, 1)
                        dve.wait_ge(c_stats_ready, 2 * r + 2)
                        apart(dve, dve_passed)
                        dve.bn_aggr(c_moments[:], c_stats[:].rearrange("p a b -> p (a b)")).then_inc(c_moments_ready, 1)
                        dve.wait_ge(c_moments_ready, r + 1)
                        dve.tensor_scalar(c_var[:], c_moments[:, 1:2], EPS, XS ** -2, ALU.add, ALU.mult)\
                           .then_inc(c_var_ready, 1)
                        dve.wait_ge(c_rstd_ready, r + 1)
                        until(dve, xn2_transposed, r)
                        dve.tensor_scalar(xn2[:, 0], x1[:, w], c_moments[:, 0:1], c_rstd[:, 0:1],
                                          ALU.subtract, ALU.mult).then_inc(xn2_ready, 1)

            pairs_of_batches(dve, steps, 2)

        @block.tensor
        def _(pe):
            pe.wait_ge(wo_lo_ready, KT)

            def steps(base, ts):
                for t in ts:
                    b, q = base + t, t % 2
                    if t < 2:
                        pe.wait_ge(ot_lo_ready, b + 1)
                        until(pe, x1_ready, b - 1)
                        for j in range(KT):
                            for part, weights in ((ot_hi, (wo_hi, wo_lo)), (ot_lo, (wo_hi,))):
                                for w in weights:
                                    for h in range(2):
                                        mm = pe.matmul(O_ps[q][:, h * 512:(h + 1) * 512],
                                                       part[:, q, j * P:(j + 1) * P], w[:, j, h * 512:(h + 1) * 512],
                                                       start=(j == 0 and part is ot_hi and w is wo_hi),
                                                       stop=(j == KT - 1 and part is ot_lo))
                        mm.then_inc(o_projected, 1)
                    if real(b - 1):
                        pe.wait_ge(xn2_ready, b)
                        until(pe, xl_ready, b - 1)
                        for k in range(KT):
                            mm = pe.transpose(X2_ps[:, k], xn2[:, 0, k * P:(k + 1) * P], ident[:])
                        mm.then_inc(xn2_transposed, 1)

            pairs_of_batches(pe, steps, 1)

        c_block.close()

        d_block = ExitStack()
        block = d_block.enter_context(nc.Block())
        G_ps, U_ps = banks[0], banks[1]
        D_ps = [banks[2][:, 0], banks[2][:, 1], banks[3][:, 0], banks[3][:, 1]]
        UPC = FB
        DPC = 2 * TPC
        SPB = NCH
        LAST = NBLK - 2

        def column(table, n):
            return table[:, n:n + 1] if isinstance(n, int) else table[:, bass.ds(n, 1)]

        def pairs_of_blocks(eng, steps):
            steps(0, 0)
            with eng.Fori(1, NBLK // 2 - 1) as i:
                steps(i * 2 * SPB, i * 2)
            steps(LAST * SPB, LAST)

        @block.sync
        def _(sp):
            for dst, src in ((g_s[:], gate_s), (u_s[:], up_s), (ds_rows[:], down_s.partition_broadcast(P))):
                sp.dma_start(dst, src).then_inc(scales_loaded, 16)

            def load_gu(a, kind, tile, q):
                until(sp, gu_ready, a - 1)
                sp.dma_start(gu_raw[:, q], (gate_w, up_w)[kind][tile].rearrange("p k f -> p (k f)"))\
                  .then_inc(gu_loaded[q], 16)

            def load_d(a, tile, q):
                until(sp, d_ready, a - 1)
                sp.dma_start(d_raw[:, q], down_w[tile]).then_inc(d_loaded[q], 16)

            for c in range(4):
                load_gu(c, c // 2, c % 2, c % 2)
            for f in range(2):
                load_d(f, f, f)

            def steps(base, block0):
                for n in range(2):
                    nxt = block0 + n + 1
                    if isinstance(nxt, int) and nxt >= NBLK:
                        continue
                    for c in range(4):
                        load_gu(nxt * 4 + c, c // 2, nxt * 2 + c % 2, c % 2)
                        if c % 2:
                            load_d(nxt * 2 + c // 2, nxt * 2 + c // 2, c // 2)

            pairs_of_blocks(sp, steps)
            sp.wait_ge(gu_ready, 4 * NBLK)
            for tile in range(NB + 2):
                if tile < NB:
                    until(sp, y_ready, 2 * (tile - 1))
                    sp.dma_start(x1_in[:, tile % 2], x1_scratch[tile]).then_inc(x1_loaded[tile % 2], 16)
                if tile >= 2:
                    sp.wait_ge(y_ready, 2 * (tile - 1))
                    sp.dma_start(out[tile - 2], acc[:, tile - 2]).then_inc(y_stored, 16)
            sp.wait_ge(y_stored, 16 * NB)

        @block.gpsimd
        def _(pool):
            def steps(base, block0):
                for t in range(2 * SPB):
                    r = base + t
                    for f in range(FB):
                        u = r * UPC + f
                        pool.wait_ge(h_hi_ready, u + 1)
                        until(pool, downed, (r - 1) * DPC)
                        pool.tensor_tensor(h_lo[:, t % 2, f], h_f[:, f % 2], h_hi[:, t % 2, f].bitcast(F32),
                                           ALU.subtract).then_inc(h_lo_ready, 1)
                    if isinstance(r, int) and r > LAST * SPB + SPB:
                        scale(t - SPB - 1)
                if isinstance(base, int) and base > 0:
                    scale(SPB - 1)

            def scale(c):
                for v in range(DPC):
                    tile, h = c * TPC + v // 2, slice(v % 2 * 512, v % 2 * 512 + 512)
                    pool.wait_ge(acc_added, ((NBLK - 1) * SPB + c) * DPC + v + 1)
                    pool.tensor_tensor(acc[:, tile, h], acc[:, tile, h], ds_rows[:, h], ALU.mult).then_inc(acc_scaled, 1)

            pool.wait_ge(scales_loaded, 48)
            pairs_of_blocks(pool, steps)

        @block.scalar
        def _(act):
            def convert(a, c, buf, before):
                act.wait_ge(gu_loaded[c % 2], 8 * (a - c % 2) + 16)
                until(act, upped, before)
                act.activation(gu_w[:, buf, c // 2, c % 2].rearrange("p k f -> p (k f)"), gu_raw[:, c % 2],
                               ACT.Copy).then_inc(gu_ready, 1)

            for c in range(4):
                convert(c, c, 0, 0)
            act.wait_ge(scales_ready, 2)

            def steps(base, block0):
                for t in range(2 * SPB):
                    r, n, c = base + t, block0 + t // SPB, t % SPB
                    for f in range(FB):
                        u = r * UPC + f
                        act.wait_ge(gated, u + 1)
                        until(act, h_ready, u - 1)
                        apart(act, act_passed)
                        act.activation(silu[:, f % 2], G_ps[:, f % 2], ACT.Silu,
                                       scale=column(g_sx, n * FB + f)).then_inc(silu_ready, 1)
                        act.wait_ge(h_ready, u + 1)
                        until(act, downed, (r - 1) * DPC)
                        act.activation(h_hi[:, t % 2, f], h_f[:, f % 2], ACT.Copy).then_inc(h_hi_ready, 1)
                    if not (isinstance(n, int) and n + 1 >= NBLK):
                        convert((n + 1) * 4 + c, c, (t // SPB + 1) % 2, n * SPB * UPC)

            pairs_of_blocks(act, steps)

        @block.vector
        def _(dve):
            dve.wait_ge(scales_loaded, 48)
            dve.tensor_scalar(g_sx[:], g_s[:], 1 / XS, None, ALU.mult).then_inc(scales_ready, 1)
            dve.tensor_scalar(u_sx[:], u_s[:], 1 / XS, None, ALU.mult).then_inc(scales_ready, 1)

            def convert(a, f, buf, before):
                dve.wait_ge(d_loaded[f], 8 * (a - f) + 16)
                until(dve, downed, before)
                dve.tensor_copy(d_w[:, buf, f], d_raw[:, f]).then_inc(d_ready, 1)

            for f in range(FB):
                convert(f, f, 0, 0)
            dve.wait_ge(scales_ready, 2)

            def add(r, c):
                for v in range(DPC):
                    tile, h = c * TPC + v // 2, slice(v % 2 * 512, v % 2 * 512 + 512)
                    dve.wait_ge(downed, r * DPC + v + 1)
                    if isinstance(r, int) and r < SPB:
                        dve.tensor_copy(acc[:, tile, h], D_ps[v % 4]).then_inc(acc_added, 1)
                    else:
                        dve.tensor_tensor(acc[:, tile, h], D_ps[v % 4], acc[:, tile, h], ALU.add)\
                           .then_inc(acc_added, 1)
                    if isinstance(r, int) and r >= (NBLK - 1) * SPB and v >= 2:
                        residual(c, v - 2)
                if isinstance(r, int) and r >= (NBLK - 1) * SPB:
                    residual(c, DPC - 2)
                    residual(c, DPC - 1)

            def residual(c, v):
                tile, h = c * TPC + v // 2, slice(v % 2 * 512, v % 2 * 512 + 512)
                dve.wait_ge(acc_scaled, c * DPC + v + 1)
                dve.wait_ge(x1_loaded[tile % 2], 16 * (tile // 2 + 1))
                dve.tensor_tensor(acc[:, tile, h], acc[:, tile, h], x1_in[:, tile % 2, h], ALU.add).then_inc(y_ready, 1)

            def steps(base, block0):
                for t in range(2 * SPB):
                    r, n, c = base + t, block0 + t // SPB, t % SPB
                    for f in range(FB):
                        u = r * UPC + f
                        dve.wait_ge(upped, u + 1)
                        dve.wait_ge(silu_ready, u + 1)
                        until(dve, h_lo_ready, u - 1)
                        dve.scalar_tensor_tensor(out=h_f[:, f % 2], in0=U_ps[:, f % 2], scalar=column(u_sx, n * FB + f),
                                                 in1=silu[:, f % 2], op0=ALU.mult, op1=ALU.mult).then_inc(h_ready, 1)
                    if real(r - 1):
                        add(r - 1, (t - 1) % SPB)
                    if c % 2 and not (isinstance(n, int) and n + 1 >= NBLK):
                        convert((n + 1) * 2 + c // 2, c // 2, (t // SPB + 1) % 2, n * SPB * DPC)
                if isinstance(base, int) and base > 0:
                    add(base + 2 * SPB - 1, SPB - 1)

            pairs_of_blocks(dve, steps)

        @block.tensor
        def _(pe):
            def down(r, c, buf, slot):
                pe.wait_ge(h_lo_ready, r * UPC + UPC)
                for v in range(DPC):
                    until(pe, acc_added, r * DPC + v - 3)
                    for f in range(FB):
                        for part in (h_hi, h_lo):
                            mm = pe.matmul(D_ps[v % 4], part[:, slot, f, v // 2 * P:(v // 2 + 1) * P],
                                           d_w[:, buf, f, v % 2 * 512:v % 2 * 512 + 512],
                                           start=(f == 0 and part is h_hi), stop=(f == FB - 1 and part is h_lo))
                    mm.then_inc(downed, 1)

            def steps(base, block0):
                for t in range(2 * SPB):
                    r, n, c, buf = base + t, block0 + t // SPB, t % SPB, t // SPB
                    if c == 0:
                        pe.wait_ge(gu_ready, n * 4 + 4)
                    tokens = slice(c * CH, (c + 1) * CH)
                    for f in range(FB):
                        u = r * UPC + f
                        for kind, (bank, done, free) in enumerate(((G_ps, gated, silu_ready), (U_ps, upped, h_ready))):
                            until(pe, free, u - 1)
                            for k in range(KT):
                                for part in (xh, xl):
                                    mm = pe.matmul(bank[:, f % 2], gu_w[:, buf, kind, f, k], part[:, k, tokens],
                                                   start=(k == 0 and part is xh), stop=(k == KT - 1 and part is xl))
                            mm.then_inc(done, 1)
                    if real(r - 1):
                        if c == 1:
                            pe.wait_ge(d_ready, n * 2 + 2)
                        down(r - 1, (c - 1) % SPB, (t - 1) // SPB % 2, (t - 1) % 2)
                if isinstance(base, int) and base > 0:
                    down(base + 2 * SPB - 1, SPB - 1, 1, 1)

            pairs_of_blocks(pe, steps)

        d_block.close()


def kernel(**inputs):
    import numpy as np
    import concourse.bacc as bacc
    from concourse.bass_utils import run_bass_kernel_spmd

    a = {n: np.asarray(v) for n, v in inputs.items()}

    def tiled(w):
        return w.reshape(-1, P, w.shape[1])

    def transposed_tiles(w):
        return w.reshape(FT, P, KT, P).transpose(0, 3, 2, 1)

    row = np.arange(P)
    pair_d = row // STATES
    arrays = {
        "x": a["x"],
        "ctx_t": a["ctx_4096"].reshape(NB, P, KT, P).transpose(0, 3, 2, 1),
        "wqkv": np.concatenate([tiled(a[f"L0_xattn_W{c}"]) for c in "qkv"]),
        "b_qk": np.stack([a["L0_xattn_bq"], a["L0_xattn_bk"]], -1).reshape(KT, P, 2).transpose(1, 0, 2),
        "b_v": a["L0_xattn_bv"].reshape(KT, P).T,
        "mix_rows": np.repeat(a["L0_xattn_interference"][:, None], DK, 1).reshape(KT, P, STATES).transpose(1, 0, 2),
        "amp": a["L0_xattn_amp"],
        "wo_t": a["L0_xattn_Wo"].T.reshape(HEADS, DK, STATES, D).transpose(0, 2, 1, 3).reshape(KT, P, D),
        "b_o": a["L0_xattn_bo"],
        "gate_w": transposed_tiles(a["L0_ffn_gate_wq"]),
        "gate_s": a["L0_ffn_gate_scale"].reshape(FT, P).T,
        "up_w": transposed_tiles(a["L0_ffn_up_wq"]),
        "up_s": a["L0_ffn_up_scale"].reshape(FT, P).T,
        "down_w": a["L0_ffn_down_wq"].T.reshape(FT, P, D),
        "down_s": a["L0_ffn_down_scale"],
        "ident_c": np.eye(P, dtype=np.float32),
        "pair_mask_c": (row[:, None] // DK == np.arange(PAIRS)).astype(np.float32),
        "fold_mask_c": (pair_d[:, None] == np.arange(HT * DK)).astype(np.float32).reshape(P, HT, DK),
        "state_eye_c": (row[:, None] % STATES == np.arange(STATES)).astype(np.float32),
    }
    nc = bacc.Bacc("TRN2", target_bir_lowering=False, num_devices=1)
    arrays = {n: np.ascontiguousarray(v) for n, v in arrays.items()}
    handles = {n: nc.dram_tensor(n, v.shape, mybir.dt.from_np(v.dtype), kind="ExternalInput").ap()
               for n, v in arrays.items()}
    out = nc.dram_tensor("out", (NB, P, D), F32, kind="ExternalOutput").ap()
    program(nc, out=out, **handles)
    result = run_bass_kernel_spmd(nc, [arrays], core_ids=[0])
    return result.results[0]["out"]
```

```python
from contextlib import ExitStack

import concourse.bass as bass
from concourse import mybir

F32 = mybir.dt.float32
F32R = mybir.dt.float32r
F16 = mybir.dt.float16
BF16 = mybir.dt.bfloat16
I32 = mybir.dt.int32
ALU = mybir.AluOpType
ACT = mybir.ActivationFunctionType
AX = mybir.AxisListType.X

P = 128
NB = 16
D = 1024
KT = D // P
HEADS, STATES, DK = 16, 4, 16
PAIRS = P // DK
HT = P // (STATES * DK)
VP = 3 * DK + 1
VS = VP + 1
STEPS = NB * KT
SCALE = DK ** -0.5
E_SHIFT = 9.704060527839234
EPS = 1e-5
HID = 3584
FT = HID // P
FB = 2
NBLK = FT // FB
CH = 512
NCH = NB * P // CH
TPC = CH // P
XS = 256.0
TOP = 2.0 ** 13


def until(eng, sem, value):
    if not isinstance(value, int) or value > 0:
        eng.wait_ge(sem, value)


def apart(eng, passed):
    eng.sem_inc(passed, 1)


def program(nc, x, ctx_t, wqkv, b_qk, b_v, mix_rows, amp, wo_t, b_o, gate_w, gate_s, up_w, up_s,
            down_w, down_s, ident_c, pair_mask_c, fold_mask_c, state_eye_c, out):
    ot_scratch = nc.dram_tensor("ot_scratch", (NB, P, KT, P), F32, kind="Internal").ap()
    x1_scratch = nc.dram_tensor("x1_scratch", (NB, P, D), F32, kind="Internal").ap()

    with ExitStack() as ctx:
        def sb(name, shape, dt, scope=ctx):
            return scope.enter_context(nc.sbuf_tensor(name, shape, dt))

        def sem(name):
            return ctx.enter_context(nc.semaphore(name))

        banks = [ctx.enter_context(nc.psum_tensor(f"banks{i}", [P, 2, 512], F32)) for i in range(4)]

        ident = sb("ident", [P, P], F32)
        pair_mask = sb("pair_mask", [P, PAIRS], F32)
        raw = sb("raw", [P, 2 * 3, D], F32)
        w_raw = raw[:, 0:3]

        b_scope = ExitStack()
        w_hi = sb("w_hi", [P, 3, KT, D], F16, b_scope)
        w_lo = sb("w_lo", [P, 3, KT, D], F16, b_scope)
        w_inv = sb("w_inv", [P, KT, 3], F32, b_scope)
        q_inv = sb("q_inv", [P, KT], F32, b_scope)
        ctx_scale = sb("ctx_scale", [P, 1], F32, b_scope)
        ctx_inv = sb("ctx_inv", [P, 1], F32, b_scope)
        kv_inv = sb("kv_inv", [P, 2, KT, 2], F32, b_scope)
        binade = sb("binade", [P, 2, 3], F32, b_scope)
        ctx_max = sb("ctx_max", [P, 1], F32, b_scope)
        ctx_all_max = sb("ctx_all_max", [P, 1], F32, b_scope)
        bias_qk = sb("bias_qk", [P, KT, 2], F32, b_scope)
        bias_v = sb("bias_v", [P, D], F32, b_scope)
        xn = sb("xn", [P, 2, D], F32, b_scope)
        xn_hi = sb("xn_hi", [P, 2, KT, P], F16, b_scope)
        xn_lo = sb("xn_lo", [P, 2, KT, P], F16, b_scope)
        ctx_raw = sb("ctx_raw", [P, KT, P], F32, b_scope)
        ctx_hi = sb("ctx_hi", [P, 2, KT, P], F16, b_scope)
        ctx_lo = sb("ctx_lo", [P, 2, KT, P], F16, b_scope)
        stats = sb("stats", [P, 2, 6], F32, b_scope)
        moments = sb("moments", [P, 2], F32, b_scope)
        var_eps = sb("var_eps", [P, 1], F32, b_scope)
        minus_half = sb("minus_half", [P, 1], F32, b_scope)
        rstd = sb("rstd", [P, 1], F32, b_scope)
        a_scope = ExitStack()
        w_f = sb("w_f", [P, 3, 3, D], F32, a_scope)
        w_scale = sb("w_scale", [P, 3, 3], F32, a_scope)
        w_inv_now = sb("w_inv_now", [P, 3], F32, a_scope)
        w_part_max = sb("w_part_max", [P, 3], F32, a_scope)
        w_all_max = sb("w_all_max", [P, 3], F32, a_scope)
        fold = sb("fold", [P, KT * P], F32, a_scope)
        fold_mask = sb("fold_mask", [P, HT, DK], F32, a_scope)
        state_eye = sb("state_eye", [P, STATES], F32, a_scope)
        mix = sb("mix", [P, KT, STATES], F32, a_scope)
        amp_sb = sb("amp_sb", [P, 1], F32, a_scope)
        amp_tenth = sb("amp_tenth", [P, 1], F32, a_scope)
        bqk_raw = sb("bqk_raw", [P, KT, 2], F32, a_scope)
        bv_raw = sb("bv_raw", [P, KT], F32, a_scope)
        bv_wide = sb("bv_wide", [P, KT, P], F32, a_scope)
        a_scope.close()
        qk_f = sb("qk_f", [P, 2, 2, P], F32, b_scope)
        qk_hi = sb("qk_hi", [P, 2, 2, P], F32R, b_scope)
        qk_lo = sb("qk_lo", [P, 2, 2, P], F32R, b_scope)
        k_wide_hi = sb("k_wide_hi", [P, 2, PAIRS, P], F32R, b_scope)
        k_wide_lo = sb("k_wide_lo", [P, 2, PAIRS, P], F32R, b_scope)
        v_f = sb("v_f", [P, 2, P], F32, b_scope)
        v_rest = sb("v_rest", [P, 2, P], F32, b_scope)
        v_parts = sb("v_parts", [P, 4, PAIRS, VS], BF16, b_scope)
        neg_max = sb("neg_max", [P, 2, PAIRS], F32, b_scope)
        s_m = sb("s_m", [P, 2, PAIRS, P], F32, b_scope)
        e_f = sb("e_f", [P, 2, PAIRS, P], F32, b_scope)
        e_hi = sb("e_hi", [P, 2, PAIRS, P], F16, b_scope)
        e_lo = sb("e_lo", [P, 2, PAIRS, P], F16, b_scope)
        o_sum = sb("o_sum", [P, 2, PAIRS, DK], F32, b_scope)
        r_den = sb("r_den", [P, 2, PAIRS, 1], F32, b_scope)
        o_tok = sb("o_tok", [P, 2, P], F32, b_scope)
        o_t = sb("o_t", [P, 2, P], F32, b_scope)
        b_scope.close()

        xh = sb("xh", [P, KT, NB * P], F16)
        xl = sb("xl", [P, KT, NB * P], F16)
        gu_w = [sb("gu_w0", [P, 2, FB, KT, P], F16)]
        g_s = sb("g_s", [P, FT], F32)
        u_s = sb("u_s", [P, FT], F32)
        g_sx = sb("g_sx", [P, FT], F32)
        u_sx = sb("u_sx", [P, FT], F32)
        c_scope = ExitStack()
        wo_raw, ot_in = raw[:, 0:4], raw[:, 4:6]
        wo_hi = sb("wo_hi", [P, KT, D], F32R, c_scope)
        wo_lo = sb("wo_lo", [P, KT, D], F32R, c_scope)
        bo_rows = sb("bo_rows", [P, D], F32, c_scope)
        ot_hi = sb("ot_hi", [P, 2, D], F32R, c_scope)
        ot_lo = sb("ot_lo", [P, 2, D], F32R, c_scope)
        x_again = sb("x_again", [P, 2, D], F32, c_scope)
        x1 = sb("x1", [P, 2, D], F32, c_scope)
        xn2 = sb("xn2", [P, 1, D], F32, c_scope)
        c_stats = sb("c_stats", [P, 2, 6], F32, c_scope)
        c_moments = sb("c_moments", [P, 2], F32, c_scope)
        c_var = sb("c_var", [P, 1], F32, c_scope)
        c_pow = sb("c_pow", [P, 1], F32, c_scope)
        c_half = sb("c_half", [P, 1], F32, c_scope)
        c_rstd = sb("c_rstd", [P, 1], F32, c_scope)
        c_scope.close()

        d_scope = ExitStack()
        acc = sb("acc", [P, NB, D], F32, d_scope)
        gu_raw, d_raw = raw[:, 0:2].bitcast(I32), raw[:, 2:4].bitcast(I32)
        gu_w.append(sb("gu_w1", [P, 2, FB, KT, P], F16, d_scope))
        d_w = sb("d_w", [P, 2, FB, D], F32R, d_scope)
        ds_rows = raw[:, 4]
        silu = raw[:, 5].rearrange("p (f t) -> p f t", t=CH)
        h_f = sb("h_f", [P, 2, CH], F32, d_scope)
        h_hi = sb("h_hi", [P, 2, FB, CH], F32R, d_scope)
        h_lo = sb("h_lo", [P, 2, FB, CH], F32R, d_scope)
        x1_in = raw[:, 0:2]
        d_scope.close()

        act_passed, dve_passed, pool_passed = sem("act_passed"), sem("dve_passed"), sem("pool_passed")
        pe_passed = sem("pe_passed")
        const_loaded = sem("const_loaded")
        w_loaded = [sem(f"w_loaded{i}") for i in range(3)]
        amp_ready, mix_ready, fold_ready = sem("amp_ready"), sem("mix_ready"), sem("fold_ready")
        bv_wide_ready = sem("bv_wide_ready")
        bias_made, bias_ready = sem("bias_made"), sem("bias_ready")
        w_folded, w_bank_free = sem("w_folded"), sem("w_bank_free")
        w_max_ready, w_all_max_ready = sem("w_max_ready"), sem("w_all_max_ready")
        w_chain, w_hi_ready, v_scaled = sem("w_chain"), sem("w_hi_ready"), sem("v_scaled")
        w_lo_ready, wv_lo_ready = sem("w_lo_ready"), sem("wv_lo_ready")
        q_inv_ready = sem("q_inv_ready")
        ctx_max_ready, ctx_all_max_ready = sem("ctx_max_ready"), sem("ctx_all_max_ready")
        ctx_chain, ctx_hi_ready, ctx_lo_ready = sem("ctx_chain"), sem("ctx_hi_ready"), sem("ctx_lo_ready")
        x_loaded = [sem("x_loaded0"), sem("x_loaded1")]
        ctx_loaded = sem("ctx_loaded")
        half_ready = sem("half_ready")
        stats_ready, moments_ready = sem("stats_ready"), sem("moments_ready")
        var_ready, rstd_ready, xn_ready = sem("var_ready"), sem("rstd_ready"), sem("xn_ready")
        xn_transposed, xn_hi_ready, xn_lo_ready = sem("xn_transposed"), sem("xn_hi_ready"), sem("xn_lo_ready")
        projected = sem("projected")
        qk_kept, qk_hi_ready, qk_lo_ready = sem("qk_kept"), sem("qk_hi_ready"), sem("qk_lo_ready")
        k_wide_hi_ready, k_wide_lo_ready, v_kept = sem("k_wide_hi_ready"), sem("k_wide_lo_ready"), sem("v_kept")
        ones_ready, v_chain, v_split = sem("ones_ready"), sem("v_chain"), sem("v_split")
        scored, max_ready, sm_ready = sem("scored"), sem("max_ready"), sem("sm_ready")
        s_transposed, e_hi_ready, e_ready = sem("s_transposed"), sem("e_hi_ready"), sem("e_ready")
        e_lo_ready, attended = sem("e_lo_ready"), sem("attended")
        o_summed, den_ready, o_ready = sem("o_summed"), sem("den_ready"), sem("o_ready")
        o_transposed, o_t_kept = sem("o_transposed"), sem("o_t_kept")
        o_t_stored = [sem("o_t_stored0"), sem("o_t_stored1")]

        bo_loaded, wo_loaded = sem("bo_loaded"), [sem(f"wo_loaded{i}") for i in range(4)]
        wo_hi_ready, wo_lo_ready = sem("wo_hi_ready"), sem("wo_lo_ready")
        ot_loaded, xa_loaded = [sem("ot_loaded0"), sem("ot_loaded1")], [sem("xa_loaded0"), sem("xa_loaded1")]
        ot_hi_ready, ot_lo_ready, xb_ready = sem("ot_hi_ready"), sem("ot_lo_ready"), sem("xb_ready")
        o_projected, x1_ready = sem("o_projected"), sem("x1_ready")
        x1_stored = [sem("x1_stored0"), sem("x1_stored1")]
        c_half_ready, c_stats_ready, c_moments_ready = sem("c_half_ready"), sem("c_stats_ready"), sem("c_moments_ready")
        c_var_ready, c_rstd_ready, xn2_ready = sem("c_var_ready"), sem("c_rstd_ready"), sem("xn2_ready")
        xn2_transposed, xh_ready, xl_ready = sem("xn2_transposed"), sem("xh_ready"), sem("xl_ready")
        scales_loaded, scales_ready = sem("scales_loaded"), sem("scales_ready")
        gu_loaded, d_loaded = [sem("gu_loaded0"), sem("gu_loaded1")], [sem("d_loaded0"), sem("d_loaded1")]
        gu_ready, d_ready = sem("gu_ready"), sem("d_ready")
        gated, upped, silu_ready = sem("gated"), sem("upped"), sem("silu_ready")
        h_ready, h_hi_ready, h_lo_ready = sem("h_ready"), sem("h_hi_ready"), sem("h_lo_ready")
        downed, acc_added, acc_scaled = sem("downed"), sem("acc_added"), sem("acc_scaled")
        x1_loaded, y_ready, y_stored = [sem("x1_loaded0"), sem("x1_loaded1")], sem("y_ready"), sem("y_stored")

        S_ps, T_ps, QKV_ps = banks[0], banks[1], banks[2]
        PV_ps = banks[3][:, 0, :]
        XT_ps = banks[3][:, 1, 0:P]
        OT_ps = banks[3][:, 1, P:2 * P]
        real = lambda r: not (isinstance(r, int) and r < 0)
        X0_ps = banks[3][:].rearrange("p b n -> p (b n)")
        S_flat = S_ps[:].rearrange("p b n -> p (b n)")
        T_flat = T_ps[:].rearrange("p b n -> p (b n)")
        S_pairs = S_flat.rearrange("p (c k) -> p c k", c=PAIRS)
        T_pairs = T_flat.rearrange("p (c k) -> p c k", c=PAIRS)
        PV_pairs = PV_ps[:, 0:PAIRS * VP].rearrange("p (c n) -> p c n", n=VP)

        W_ps = (S_pairs, T_pairs, QKV_ps[:].rearrange("p b (c k) -> p (b c) k", k=P))

        def other_tiles(eng, tiles):
            with eng.Fori(0, (KT - 2) // 3) as i:
                for g in range(3):
                    tiles(3 * i + 2 + g, (2 + g) % 3)

        w_f_tiles = w_f[:].rearrange("p g m (k f) -> p g m k f", f=P)
        w_inv_flat = w_inv[:].rearrange("p j m -> p (j m)")

        def at3(j):
            return slice(3 * j, 3 * j + 3) if isinstance(j, int) else bass.ds(3 * j, 3)

        def at(j):
            return slice(j * P, j * P + P) if isinstance(j, int) else bass.ds(j * P, P)

        ab_scope = ExitStack()
        block = ab_scope.enter_context(nc.Block())

        @block.sync
        def _(sp):
            small = [(ident[:], ident_c), (pair_mask[:], pair_mask_c), (fold_mask[:], fold_mask_c),
                     (state_eye[:], state_eye_c), (mix[:], mix_rows), (bqk_raw[:], b_qk), (bv_raw[:], b_v),
                     (amp_sb[:], amp.partition_broadcast(P))]
            for dst, src in small:
                sp.dma_start(dst, src).then_inc(const_loaded, 16)
            for c in range(3):
                sp.dma_start(w_raw[:, c], wqkv[c]).then_inc(w_loaded[c], 16)
            sp.dma_start(xn[:, 0], x[0]).then_inc(x_loaded[0], 16)
            sp.dma_start(ctx_raw[:], ctx_t[0]).then_inc(ctx_loaded, 16)
            sp.dma_start(xn[:, 1], x[1]).then_inc(x_loaded[1], 16)
            with sp.Fori(1, KT) as j:
                for c in range(3):
                    sp.wait_ge(w_folded, 3 * j + c - 2)
                    sp.dma_start(w_raw[:, c], wqkv[3 * j + c]).then_inc(w_loaded[c], 16)
            sp.wait_ge(ctx_lo_ready, 1)
            sp.dma_start(ctx_raw[:], ctx_t[1]).then_inc(ctx_loaded, 16)

            def steps(base, batch, ts):
                for t in ts:
                    b, j = batch + t // KT, t % KT
                    if j == 0 and t < 16 and not (isinstance(b, int) and b + 2 >= NB):
                        sp.wait_ge(xn_transposed, KT * b + KT)
                        sp.dma_start(xn[:, t // KT], x[b + 2]).then_inc(x_loaded[t // KT], 16)
                    if j == 5 and t < 16 and not (isinstance(b, int) and b + 2 >= NB):
                        sp.wait_ge(ctx_lo_ready, b + 2)
                        sp.dma_start(ctx_raw[:], ctx_t[b + 2]).then_inc(ctx_loaded, 16)
                    if isinstance(b, int) and t == 8 and b == NB - 1:
                        for c in range(4):
                            sp.dma_start(wo_raw[:, c], wo_t[c]).then_inc(wo_loaded[c], 16)
                        for n in range(2):
                            sp.dma_start(ot_in[:, n], ot_scratch[n].rearrange("p k t -> p (k t)"))\
                              .then_inc(ot_loaded[n], 16)
                    r, w = base + t - 5, (t - 5) % 2
                    if isinstance(r, int) and r < 0:
                        continue
                    rb, rj = batch + (t - 5) // KT, (t - 5) % KT
                    sp.wait_ge(o_t_kept, r + 1)
                    sp.dma_start(ot_scratch[rb, :, rj, :], o_t[:, w]).then_inc(o_t_stored[w], 16)

            steps(0, 0, range(16))
            with sp.Fori(1, NB // 2 - 1) as i:
                steps(i * 16, i * 2, range(16))
            steps(STEPS - 16, NB - 2, range(16))
            steps(STEPS - 16, NB - 2, range(16, 21))
            for q in o_t_stored:
                sp.wait_ge(q, 16 * STEPS // 2)

        @block.gpsimd
        def _(pool):
            pool.memset(minus_half[:], -0.5).then_inc(half_ready, 1)
            pool.wait_ge(half_ready, 1)

            def root(n):
                pool.wait_ge(var_ready, n + 1)
                pool.tensor_tensor(rstd[:], var_eps[:], minus_half[:], ALU.pow).then_inc(rstd_ready, 1)

            def ctx_maximum(n):
                pool.wait_ge(ctx_max_ready, n + 1)
                apart(pool, pool_passed)
                pool.partition_all_reduce(ctx_all_max[:], ctx_max[:], P, bass.bass_isa.ReduceOp.max)\
                    .then_inc(ctx_all_max_ready, 1)

            root(0)

            def tiles(j, g):
                pool.wait_ge(w_max_ready, j + 1)
                until(pool, w_chain, 6 * j)
                apart(pool, pool_passed)
                pool.partition_all_reduce(w_all_max[:], w_part_max[:], P, bass.bass_isa.ReduceOp.max)\
                    .then_inc(w_all_max_ready, 1)
                if real(j - 1):
                    low_v(j - 1, (g + 2) % 3)

            def low_v(j, g):
                pool.wait_ge(v_scaled, j + 1)
                apart(pool, pool_passed)
                pool.tensor_tensor(w_lo[:, 2, :, at(j)], w_f_tiles[:, g, 2], w_hi[:, 2, :, at(j)], ALU.subtract)\
                    .then_inc(wv_lo_ready, 1)

            ctx_maximum(0)
            root(1)
            tiles(0, 0)
            tiles(1, 1)
            other_tiles(pool, tiles)
            low_v(KT - 1, (KT - 1) % 3)
            pool.wait_ge(w_folded, 3 * KT)
            pool.wait_ge(wv_lo_ready, KT + 1)
            pool.wait_ge(w_lo_ready, 2 * KT + 2)
            pool.wait_ge(bias_made, 1)
            pool.memset(v_parts[:, :, :, VP - 1:VP], 1.0).then_inc(ones_ready, 1)

            def steps(base, batch, ts):
                for t in ts:
                    s, b, j = base + t, batch + t // KT, t % KT
                    if t < 16:
                        pool.wait_ge(qk_lo_ready, s + 1)
                        until(pool, scored, s - 1)
                        pool.tensor_tensor(k_wide_lo[:, t % 2],
                                           qk_lo[:, t % 2, 1].bitcast(F32).unsqueeze(1).to_broadcast([P, PAIRS, P]),
                                           pair_mask[:].unsqueeze(2).to_broadcast([P, PAIRS, P]), ALU.mult)\
                            .then_inc(k_wide_lo_ready, 1)
                        pool.wait_ge(v_kept, s + 1)
                        until(pool, attended, s - 3)
                        part = [v_parts[:, t % 4, :, DK * q:DK * (q + 1)] for q in range(3)]
                        whole = v_f[:, t % 2].rearrange("p (c d) -> p c d", d=DK)
                        apart(pool, pool_passed)
                        rest = v_rest[:, t % 2].rearrange("p (c d) -> p c d", d=DK)
                        pool.tensor_copy(part[0], whole).then_inc(v_chain, 1)
                        pool.wait_ge(v_chain, 3 * s + 1)
                        pool.tensor_tensor(rest, whole, part[0], ALU.subtract).then_inc(v_chain, 1)
                        pool.wait_ge(v_chain, 3 * s + 2)
                        apart(pool, pool_passed)
                        pool.tensor_copy(part[1], rest).then_inc(v_chain, 1)
                        pool.wait_ge(v_chain, 3 * s + 3)
                        pool.tensor_tensor(part[2], rest, part[1], ALU.subtract).then_inc(v_split, 1)
                    r = s - 2
                    if not (isinstance(r, int) and r < 0) and t < 18:
                        pool.wait_ge(e_ready, r + 1)
                        pool.wait_ge(e_hi_ready, r + 1)
                        until(pool, attended, r - 1)
                        pool.tensor_tensor(e_lo[:, t % 2], e_f[:, t % 2], e_hi[:, t % 2],
                                           ALU.subtract).then_inc(e_lo_ready, 1)
                    if j == 1 and t < 16 and not (isinstance(b, int) and b + 1 >= NB):
                        ctx_maximum(b + 1)
                    if j == 5 and t < 16 and not (isinstance(b, int) and b + 2 >= NB):
                        root(b + 2)

            steps(0, 0, range(16))
            with pool.Fori(1, NB // 2 - 1) as i:
                steps(i * 16, i * 2, range(16))
            steps(STEPS - 16, NB - 2, range(18))

        @block.scalar
        def _(act):
            act.sem_inc(w_bank_free, 3)
            act.sem_inc(w_lo_ready, 2)
            act.sem_inc(wv_lo_ready, 1)

            def tiles(j, g):
                for m in range(3):
                    act.wait_ge(w_folded, 3 * j + m + 1)
                    if m < 2:
                        until(act, w_lo_ready, 2 * (j - 2) + m + 1)
                    else:
                        until(act, wv_lo_ready, j - 1)
                    act.activation(w_f_tiles[:, g, m], W_ps[m], ACT.Copy).then_inc(w_bank_free, 1)
                if real(j - 1):
                    highs(j - 1, (g + 2) % 3)

            def highs(j, g):
                act.wait_ge(w_chain, 6 * j + 6)
                apart(act, act_passed)
                for m in (2, 0, 1):
                    act.activation(w_hi[:, m, :, at(j)], w_f_tiles[:, g, m], ACT.Copy, scale=w_scale[:, g, m:m + 1])\
                       .then_inc(w_hi_ready, 1)
                    if m == 2:
                        act.wait_ge(w_hi_ready, 3 * j + 1)
                        act.activation(w_f[:, g, 2], w_f[:, g, 2], ACT.Copy, scale=w_scale[:, g, 2:3])\
                           .then_inc(v_scaled, 1)

            def keep_xn(n, slot, j, before):
                act.wait_ge(xn_transposed, n + 1)
                if j == 0:
                    until(act, projected, before)
                act.activation(xn_hi[:, slot, j], XT_ps, ACT.Copy).then_inc(xn_hi_ready, 1)

            def keep_ctx(n, slot, before):
                act.wait_ge(ctx_chain, 6 * n + 5)
                until(act, projected, before)
                act.activation(ctx_hi[:, slot], ctx_raw[:], ACT.Copy, scale=ctx_scale[:, 0:1])\
                   .then_inc(ctx_hi_ready, 1)

            tiles(0, 0)
            tiles(1, 1)
            act.wait_ge(xn_transposed, KT)
            act.activation(xn_hi[:, 0].rearrange("p k t -> p (k t)"), X0_ps, ACT.Copy).then_inc(xn_hi_ready, KT)
            keep_ctx(0, 0, 0)
            other_tiles(act, tiles)
            highs(KT - 1, (KT - 1) % 3)
            act.wait_ge(ctx_chain, 6)
            act.wait_ge(w_lo_ready, 2 * KT + 2)
            act.wait_ge(wv_lo_ready, KT + 1)
            act.wait_ge(q_inv_ready, 1)
            act.wait_ge(bias_ready, 2)

            def steps(base, batch, ts):
                for t in ts:
                    s, b, j = base + t, batch + t // KT, t % KT
                    r = s - 5
                    if not (isinstance(r, int) and r < 0):
                        w = (t - 5) % 2
                        act.wait_ge(o_transposed, r + 1)
                        until(act, o_t_stored[w], 8 * (r - w))
                        act.activation(o_t[:, w], OT_ps, ACT.Copy).then_inc(o_t_kept, 1)
                    if t < 16:
                        act.wait_ge(projected, s + 1)
                        until(act, qk_lo_ready, s - 1)
                        act.activation(qk_f[:, t % 2, 0], QKV_ps[:, t % 2, 0:P], ACT.Identity, scale=q_inv[:, j:j + 1],
                                       bias=bias_qk[:, j, 0:1]).then_inc(qk_kept, 1)
                        act.activation(qk_f[:, t % 2, 1], QKV_ps[:, t % 2, P:2 * P], ACT.Identity,
                                       scale=kv_inv[:, t // KT, j, 0:1], bias=bias_qk[:, j, 1:2]).then_inc(qk_kept, 1)
                        if not (isinstance(b, int) and b + 1 >= NB):
                            keep_xn(s + KT, (t // KT + 1) % 2, j, KT * b)
                        act.wait_ge(qk_kept, 2 * s + 2)
                        until(act, scored, s - 1)
                        act.activation(qk_hi[:, t % 2], qk_f[:, t % 2], ACT.Copy).then_inc(qk_hi_ready, 1)
                        if not (isinstance(b, int) and b + 1 >= NB):
                            if j == 3:
                                keep_ctx(b + 1, (t // KT + 1) % 2, KT * b)
                    r = s - 2
                    if not (isinstance(r, int) and r < 0) and t < 18:
                        act.wait_ge(s_transposed, r + 1)
                        until(act, attended, r - 1)
                        act.activation(e_hi[:, t % 2], T_pairs, ACT.Exp, bias=E_SHIFT, scale=SCALE)\
                           .then_inc(e_hi_ready, 1)
                        until(act, e_lo_ready, r - 1)
                        act.activation(e_f[:, t % 2], T_pairs, ACT.Exp, bias=E_SHIFT, scale=SCALE)\
                           .then_inc(e_ready, 1)

            steps(0, 0, range(16))
            with act.Fori(1, NB // 2 - 1) as i:
                steps(i * 16, i * 2, range(16))
            steps(STEPS - 16, NB - 2, range(21))

        @block.vector
        def _(dve):
            dve.wait_ge(const_loaded, 16 * 8)
            dve.tensor_scalar(amp_tenth[:], amp_sb[:], 0.1, None, ALU.mult).then_inc(amp_ready, 1)
            dve.wait_ge(amp_ready, 1)
            dve.scalar_tensor_tensor(out=mix[:], in0=mix[:], scalar=amp_tenth[:, 0:1],
                                     in1=state_eye[:].unsqueeze(1).to_broadcast([P, KT, STATES]),
                                     op0=ALU.mult, op1=ALU.add).then_inc(mix_ready, 1)
            dve.wait_ge(mix_ready, 1)
            for j in range(KT):
                for h in range(HT):
                    width = STATES * DK
                    dve.tensor_tensor(
                        fold[:, j * P + h * width:j * P + (h + 1) * width].rearrange("p (m d) -> p m d", d=DK),
                        mix[:, j].unsqueeze(2).to_broadcast([P, STATES, DK]),
                        fold_mask[:, h:h + 1, :].to_broadcast([P, STATES, DK]), ALU.mult).then_inc(fold_ready, 1)
            dve.tensor_tensor(bv_wide[:], bv_raw[:].unsqueeze(2).to_broadcast([P, KT, P]),
                              ident[:, 0:1].unsqueeze(1).to_broadcast([P, KT, P]), ALU.bypass)\
               .then_inc(bv_wide_ready, 1)

            def moments_of(n, slot):
                if isinstance(n, int):
                    dve.wait_ge(x_loaded[slot], 16 * (n // 2 + 1))
                else:
                    dve.wait_ge(x_loaded[slot], 8 * (n - slot + 2))
                for q in range(2):
                    dve.bn_stats(stats[:, q], xn[:, slot, q * 512:(q + 1) * 512]).then_inc(stats_ready, 1)
                dve.wait_ge(stats_ready, 2 * n + 2)
                apart(dve, dve_passed)
                dve.bn_aggr(moments[:], stats[:].rearrange("p a b -> p (a b)")).then_inc(moments_ready, 1)
                dve.wait_ge(moments_ready, n + 1)
                until(dve, rstd_ready, n)
                dve.tensor_scalar(var_eps[:], moments[:, 1:2], EPS, XS ** -2, ALU.add, ALU.mult)\
                   .then_inc(var_ready, 1)

            def normalise(n, slot):
                dve.wait_ge(rstd_ready, n + 1)
                dve.tensor_scalar(xn[:, slot], xn[:, slot], moments[:, 0:1], rstd[:, 0:1],
                                  ALU.subtract, ALU.mult).then_inc(xn_ready, 1)

            def power_of_two(largest, scale, inv, chain, n):
                wide = largest.shape[-1]
                dve.tensor_scalar(binade[:, 0, 0:wide].bitcast(I32), largest.bitcast(I32), 0x7f800000, None,
                                  ALU.bitwise_and).then_inc(chain, 1)
                dve.wait_ge(chain, 6 * n + 1)
                dve.tensor_scalar(binade[:, 1, 0:wide], binade[:, 0, 0:wide], 2.0 ** -100, None, ALU.max)\
                   .then_inc(chain, 1)
                dve.wait_ge(chain, 6 * n + 2)
                dve.reciprocal(scale, binade[:, 1, 0:wide]).then_inc(chain, 1)
                dve.wait_ge(chain, 6 * n + 3)
                if not isinstance(n, int):
                    apart(dve, dve_passed)
                dve.tensor_scalar(inv, binade[:, 1, 0:wide], 1 / TOP, None, ALU.mult).then_inc(chain, 1)
                dve.tensor_scalar(scale, scale, TOP, None, ALU.mult).then_inc(chain, 1)
                dve.wait_ge(chain, 6 * n + 5)

            def ctx_maximum(n):
                dve.wait_ge(ctx_loaded, 16 * (n + 1))
                until(dve, ctx_all_max_ready, n)
                dve.tensor_reduce(ctx_max[:], ctx_raw[:].rearrange("p k t -> p (k t)"), AX, ALU.max,
                                  apply_absolute_value=True).then_inc(ctx_max_ready, 1)

            def ctx_scaling(n):
                dve.wait_ge(ctx_all_max_ready, n + 1)
                until(dve, ctx_hi_ready, n)
                power_of_two(ctx_all_max[:], ctx_scale[:], ctx_inv[:], ctx_chain, n)

            def kv_unscaling(slot):
                dve.tensor_scalar(kv_inv[:, slot], w_inv[:, :, 1:3], ctx_inv[:, 0:1], None, ALU.mult)\
                   .then_inc(ctx_chain, 1)

            def ctx_low(n, slot):
                dve.wait_ge(ctx_hi_ready, n + 1)
                dve.scalar_tensor_tensor(out=ctx_lo[:, slot], in0=ctx_raw[:], scalar=ctx_scale[:, 0:1],
                                         in1=ctx_hi[:, slot], op0=ALU.mult, op1=ALU.subtract).then_inc(ctx_lo_ready, 1)

            def low_xn(n, slot, j):
                dve.wait_ge(xn_hi_ready, n + 1)
                dve.tensor_tensor(xn_lo[:, slot, j], XT_ps, xn_hi[:, slot, j], ALU.subtract).then_inc(xn_lo_ready, 1)

            def tiles(j, g):
                dve.wait_ge(w_bank_free, 3 * j + 6)
                dve.tensor_reduce(w_part_max[:], w_f[:, g], AX, ALU.max, apply_absolute_value=True)\
                   .then_inc(w_max_ready, 1)
                if real(j - 1):
                    lows(j - 1, (g + 2) % 3)
                dve.wait_ge(w_all_max_ready, j + 1)
                power_of_two(w_all_max[:], w_scale[:, g], w_inv_now[:], w_chain, j)
                apart(dve, dve_passed)
                dve.tensor_copy(w_inv_flat[:, at3(j)], w_inv_now[:]).then_inc(w_chain, 1)

            def lows(j, g):
                for m in range(2):
                    dve.wait_ge(w_hi_ready, 3 * j + 2 + m)
                    apart(dve, dve_passed)
                    dve.scalar_tensor_tensor(out=w_lo[:, m, :, at(j)], in0=w_f_tiles[:, g, m],
                                             scalar=w_scale[:, g, m:m + 1], in1=w_hi[:, m, :, at(j)],
                                             op0=ALU.mult, op1=ALU.subtract).then_inc(w_lo_ready, 1)

            moments_of(0, 0)
            normalise(0, 0)
            dve.wait_ge(bias_made, 1)
            dve.tensor_copy(bias_qk[:], QKV_ps[:, 0, 0:2 * KT].rearrange("p (j m) -> p j m", m=2))\
               .then_inc(bias_ready, 1)
            dve.tensor_copy(bias_v[:], banks[3][:].rearrange("p b n -> p (b n)")).then_inc(bias_ready, 1)
            dve.wait_ge(bias_ready, 2)
            ctx_maximum(0)
            dve.wait_ge(xn_ready, 1)
            moments_of(1, 1)
            ctx_scaling(0)
            normalise(1, 1)
            dve.wait_ge(xn_ready, 2)
            tiles(0, 0)
            tiles(1, 1)
            dve.wait_ge(xn_hi_ready, KT)
            dve.tensor_tensor(xn_lo[:, 0].rearrange("p k t -> p (k t)"), X0_ps,
                              xn_hi[:, 0].rearrange("p k t -> p (k t)"), ALU.subtract).then_inc(xn_lo_ready, KT)
            ctx_low(0, 0)
            other_tiles(dve, tiles)
            dve.wait_ge(w_chain, 6 * KT)
            dve.tensor_scalar(q_inv[:], w_inv[:, :, 0], 1 / XS, None, ALU.mult).then_inc(q_inv_ready, 1)
            kv_unscaling(0)
            lows(KT - 1, (KT - 1) % 3)
            dve.wait_ge(w_lo_ready, 2 * KT + 2)
            dve.wait_ge(wv_lo_ready, KT + 1)

            def steps(base, batch, ts):
                for t in ts:
                    s, b, j = base + t, batch + t // KT, t % KT
                    if t < 16:
                        dve.wait_ge(qk_kept, 2 * s + 2)
                        until(dve, v_split, s - 1)
                        dve.scalar_tensor_tensor(out=v_f[:, t % 2], in0=QKV_ps[:, t % 2, 2 * P:3 * P],
                                                 scalar=kv_inv[:, t // KT, j, 1:2], in1=bias_v[:, j * P:(j + 1) * P],
                                                 op0=ALU.mult, op1=ALU.add).then_inc(v_kept, 1)
                        if not (isinstance(b, int) and b + 1 >= NB):
                            low_xn(s + KT, (t // KT + 1) % 2, j)
                        dve.wait_ge(qk_hi_ready, s + 1)
                        until(dve, scored, s - 1)
                        dve.tensor_tensor(qk_lo[:, t % 2], qk_f[:, t % 2], qk_hi[:, t % 2].bitcast(F32), ALU.subtract)\
                           .then_inc(qk_lo_ready, 1)
                        dve.tensor_tensor(k_wide_hi[:, t % 2],
                                          qk_hi[:, t % 2, 1].bitcast(F32).unsqueeze(1).to_broadcast([P, PAIRS, P]),
                                          pair_mask[:].unsqueeze(2).to_broadcast([P, PAIRS, P]), ALU.mult)\
                           .then_inc(k_wide_hi_ready, 1)
                        if not (isinstance(b, int) and b + 1 >= NB):
                            if j == 1:
                                ctx_maximum(b + 1)
                            if j == 2:
                                ctx_scaling(b + 1)
                                kv_unscaling((t // KT + 1) % 2)
                            if j == 4:
                                ctx_low(b + 1, (t // KT + 1) % 2)
                    r = s - 1
                    if not (isinstance(r, int) and r < 0) and t < 17:
                        dve.wait_ge(scored, r + 1)
                        until(dve, sm_ready, r - 1)
                        dve.tensor_reduce(neg_max[:, (t - 1) % 2], S_pairs, AX, ALU.max, negate=True)\
                           .then_inc(max_ready, 1)
                        dve.wait_ge(max_ready, r + 1)
                        until(dve, s_transposed, r - 1)
                        dve.tensor_tensor(s_m[:, (t - 1) % 2], S_pairs,
                                          neg_max[:, (t - 1) % 2].unsqueeze(2).to_broadcast([P, PAIRS, P]),
                                          ALU.add).then_inc(sm_ready, 1)
                    r = s - 3
                    if not (isinstance(r, int) and r < 0) and t < 19:
                        w = (t - 3) % 2
                        dve.wait_ge(attended, r + 1)
                        until(dve, o_ready, r - 1)
                        dve.tensor_reduce(o_sum[:, w], PV_pairs[:, :, 0:3 * DK].rearrange("p c (q d) -> p c d q", q=3),
                                          AX, ALU.add).then_inc(o_summed, 1)
                        dve.reciprocal(r_den[:, w], PV_pairs[:, :, VP - 1:VP]).then_inc(den_ready, 1)
                        dve.wait_ge(o_summed, r + 1)
                        dve.wait_ge(den_ready, r + 1)
                        until(dve, o_transposed, r - 1)
                        dve.tensor_tensor(o_tok[:, w].rearrange("p (c d) -> p c d", d=DK), o_sum[:, w],
                                          r_den[:, w].to_broadcast([P, PAIRS, DK]), ALU.mult).then_inc(o_ready, 1)
                    if t < 16 and not (isinstance(b, int) and b + 2 >= NB):
                        if j == 3:
                            moments_of(b + 2, t // KT)
                        if j == 6:
                            normalise(b + 2, t // KT)

            steps(0, 0, range(16))
            with dve.Fori(1, NB // 2 - 1) as i:
                steps(i * 16, i * 2, range(16))
            steps(STEPS - 16, NB - 2, range(19))

        @block.tensor
        def _(pe):
            pe.wait_ge(const_loaded, 16 * 8)
            pe.wait_ge(fold_ready, KT * HT)
            for j in range(KT):
                pe.matmul(QKV_ps[:, 0, 2 * j:2 * j + 2], fold[:, at(j)], bqk_raw[:, j, :], start=True, stop=True)
            pe.wait_ge(bv_wide_ready, 1)
            for j in range(KT):
                mm = pe.matmul(banks[3][:, j // 4, (j % 4) * P:(j % 4 + 1) * P], bv_wide[:, j, :], fold[:, at(j)],
                               start=True, stop=True)
            mm.then_inc(bias_made, 1)

            def tiles(j, g):
                for m in range(3):
                    pe.wait_ge(w_loaded[m], 16 * j + 16)
                    if isinstance(j, int) and j == 0 and m == 2:
                        pe.wait_ge(bias_ready, 1)
                    pe.wait_ge(w_bank_free, 3 * j + m + 1)
                    apart(pe, pe_passed)
                    for k in range(KT):
                        mm = pe.matmul(W_ps[m][:, k, :], w_raw[:, m, k * P:(k + 1) * P],
                                       fold[:, at(j)], start=True, stop=True)
                    mm.then_inc(w_folded, 1)

            tiles(0, 0)
            tiles(1, 1)
            pe.wait_ge(xn_ready, 1)
            pe.wait_ge(bias_ready, 2)
            for k in range(KT):
                mm = pe.transpose(X0_ps[:, at(k)], xn[:, 0, at(k)], ident[:])
            mm.then_inc(xn_transposed, KT)
            other_tiles(pe, tiles)
            pe.wait_ge(w_bank_free, 3 * KT + 3)

            def transpose_xn(n, slot, j):
                until(pe, xn_lo_ready, n)
                until(pe, o_t_kept, n - KT - 4)
                pe.transpose(XT_ps, xn[:, slot, j * P:(j + 1) * P], ident[:]).then_inc(xn_transposed, 1)

            def steps(base, batch, ts):
                for t in ts:
                    s, b, j = base + t, batch + t // KT, t % KT
                    here = t // KT % 2
                    r = s - 5
                    if not (isinstance(r, int) and r < 0):
                        pe.wait_ge(o_ready, r + 1)
                        until(pe, o_t_kept, r)
                        if not (isinstance(r, int) and s + KT > STEPS):
                            pe.wait_ge(xn_lo_ready, s + KT)
                        pe.transpose(OT_ps, o_tok[:, (t - 5) % 2], ident[:]).then_inc(o_transposed, 1)
                    if t < 16:
                        if j == 0:
                            pe.wait_ge(xn_lo_ready, KT * (b + 1))
                            pe.wait_ge(ctx_lo_ready, b + 1)
                        if isinstance(b, int) and b == 0:
                            pe.wait_ge(w_lo_ready, 2 * (j + 2))
                            pe.wait_ge(wv_lo_ready, j + 2)
                        cols = slice(j * P, (j + 1) * P)
                        until(pe, v_kept, s - 1)
                        for m, (src_hi, src_lo) in enumerate(((xn_hi, xn_lo), (ctx_hi, ctx_lo), (ctx_hi, ctx_lo))):
                            for k in range(KT):
                                for src, w in ((src_hi, w_hi), (src_lo, w_hi), (src_hi, w_lo)):
                                    act_tile, w_tile = src[:, here, k], w[:, m, k, cols]
                                    mm = pe.matmul(QKV_ps[:, t % 2, m * P:(m + 1) * P],
                                                   w_tile if m < 2 else act_tile, act_tile if m < 2 else w_tile,
                                                   start=(k == 0 and src is src_hi and w is w_hi),
                                                   stop=(k == KT - 1 and w is w_lo))
                        mm.then_inc(projected, 1)
                        if not (isinstance(b, int) and b + 1 >= NB):
                            if j == 0:
                                pe.wait_ge(xn_ready, b + 2)
                            transpose_xn(s + KT, 1 - here, j)
                    r = s - 1
                    if not (isinstance(r, int) and r < 0) and t < 17:
                        pe.wait_ge(k_wide_hi_ready, r + 1)
                        pe.wait_ge(k_wide_lo_ready, r + 1)
                        until(pe, sm_ready, r)
                        for q, k_wide in ((qk_hi, k_wide_hi), (qk_lo, k_wide_hi), (qk_hi, k_wide_lo)):
                            for h in range(2):
                                mm = pe.matmul(S_ps[:, h], q[:, (t - 1) % 2, 0],
                                               k_wide[:, (t - 1) % 2, 4 * h:4 * h + 4].rearrange("p c k -> p (c k)"),
                                               start=(q is qk_hi and k_wide is k_wide_hi), stop=(k_wide is k_wide_lo))
                        mm.then_inc(scored, 1)
                    r = s - 2
                    if not (isinstance(r, int) and r < 0) and t < 18:
                        pe.wait_ge(sm_ready, r + 1)
                        until(pe, e_ready, r)
                        for c in range(PAIRS):
                            mm = pe.transpose(T_pairs[:, c, :], s_m[:, t % 2, c, :], ident[:])
                        mm.then_inc(s_transposed, 1)
                    r = s - 3
                    if not (isinstance(r, int) and r < 0) and t < 19:
                        pe.wait_ge(e_hi_ready, r + 1)
                        pe.wait_ge(e_lo_ready, r + 1)
                        pe.wait_ge(v_split, r + 1)
                        if isinstance(r, int) and r == 0:
                            pe.wait_ge(ones_ready, 1)
                        until(pe, o_summed, r)
                        until(pe, den_ready, r)
                        for c in range(PAIRS):
                            for e in (e_hi, e_lo):
                                mm = pe.matmul(PV_pairs[:, c, :], e[:, (t - 3) % 2, c, :],
                                               v_parts[:, (t - 3) % 4, c, 0:VP], start=(e is e_hi), stop=(e is e_lo))
                        mm.then_inc(attended, 1)

            steps(0, 0, range(16))
            with pe.Fori(1, NB // 2 - 1) as i:
                steps(i * 16, i * 2, range(16))
            steps(STEPS - 16, NB - 2, range(21))

        ab_scope.close()

        c_block = ExitStack()
        block = c_block.enter_context(nc.Block())
        O_ps = [b[:].rearrange("p b n -> p (b n)") for b in banks[0:2]]
        X2_ps = banks[2][:].rearrange("p b (k t) -> p (b k) t", t=P)
        xh_b = xh[:].rearrange("p k (b t) -> p k b t", t=P)
        xl_b = xl[:].rearrange("p k (b t) -> p k b t", t=P)

        def pairs_of_batches(eng, steps, tail):
            steps(0, range(2))
            with eng.Fori(1, NB // 2) as i:
                steps(i * 2, range(2))
            steps(NB - 2, range(2, 2 + tail))

        @block.sync
        def _(sp):
            sp.dma_start(bo_rows[:], b_o.partition_broadcast(P)).then_inc(bo_loaded, 16)
            for j in range(4, KT):
                sp.wait_ge(wo_lo_ready, j - 3)
                sp.dma_start(wo_raw[:, j % 4], wo_t[j]).then_inc(wo_loaded[j % 4], 16)

            def steps(base, ts):
                for t in ts:
                    b, q = base + t, t % 2
                    if t < 2:
                        if not isinstance(b, int):
                            sp.wait_ge(ot_lo_ready, b - 1)
                            sp.dma_start(ot_in[:, q], ot_scratch[b].rearrange("p k t -> p (k t)"))\
                              .then_inc(ot_loaded[q], 16)
                        until(sp, x1_ready, b - 1)
                        sp.dma_start(x_again[:, q], x[b]).then_inc(xa_loaded[q], 16)
                    if real(b - 2):
                        sp.wait_ge(x1_ready, b - 1)
                        sp.dma_start(x1_scratch[b - 2], x1[:, q]).then_inc(x1_stored[q], 16)

            def first_of_d():
                sp.dma_start(g_s[:], gate_s).then_inc(scales_loaded, 16)
                sp.dma_start(u_s[:], up_s).then_inc(scales_loaded, 16)
                sp.wait_ge(wo_lo_ready, KT)
                for c in range(4):
                    until(sp, gu_ready, c - 1)
                    sp.dma_start(gu_raw[:, c % 2], (gate_w, up_w)[c // 2][c % 2].rearrange("p k f -> p (k f)"))\
                      .then_inc(gu_loaded[c % 2], 16)

            pairs_of_batches(sp, steps, 0)
            first_of_d()
            steps(NB - 2, range(2, 4))
            for q in range(2):
                sp.wait_ge(x1_stored[q], 16 * NB // 2)

        @block.gpsimd
        def _(pool):
            pool.memset(c_half[:], -0.5).then_inc(c_half_ready, 1)
            pool.wait_ge(c_half_ready, 1)
            pool.wait_ge(bo_loaded, 16)

            def steps(base, ts):
                for t in ts:
                    b, q = base + t, t % 2
                    if t < 2:
                        pool.wait_ge(xa_loaded[q], 8 * (b - q) + 16)
                        pool.tensor_tensor(x_again[:, q], x_again[:, q], bo_rows[:], ALU.add).then_inc(xb_ready, 1)
                    if real(b - 1):
                        pool.wait_ge(c_var_ready, b)
                        pool.tensor_tensor(c_rstd[:], c_var[:], c_half[:], ALU.pow).then_inc(c_rstd_ready, 1)

            pairs_of_batches(pool, steps, 1)

        @block.scalar
        def _(act):
            def split_wo():
                for j in range(KT):
                    act.wait_ge(wo_loaded[j % 4], 16 * (j // 4 + 1))
                    act.activation(wo_hi[:, j], wo_raw[:, j % 4], ACT.Copy).then_inc(wo_hi_ready, 1)

            def steps(base, ts):
                for t in ts:
                    b, q = base + t, t % 2
                    if t < 2:
                        act.wait_ge(ot_loaded[q], 8 * (b - q) + 16)
                        until(act, o_projected, b - 1)
                        act.activation(ot_hi[:, q], ot_in[:, q], ACT.Copy).then_inc(ot_hi_ready, 1)
                        if isinstance(b, int) and b == 0:
                            split_wo()
                    if real(b - 2):
                        act.wait_ge(xn2_transposed, b - 1)
                        apart(act, act_passed)
                        act.activation(xh_b[:, :, b - 2, :], X2_ps, ACT.Copy).then_inc(xh_ready, 1)

            pairs_of_batches(act, steps, 0)
            for c in range(4):
                act.wait_ge(gu_loaded[c % 2], 16 * (c // 2 + 1))
                act.activation(gu_w[0][:, c // 2, c % 2].rearrange("p k f -> p (k f)"), gu_raw[:, c % 2], ACT.Copy)\
                   .then_inc(gu_ready, 1)
            steps(NB - 2, range(2, 4))

        @block.vector
        def _(dve):
            def split_wo():
                for j in range(KT):
                    dve.wait_ge(wo_hi_ready, j + 1)
                    dve.tensor_tensor(wo_lo[:, j], wo_raw[:, j % 4], wo_hi[:, j].bitcast(F32), ALU.subtract)\
                       .then_inc(wo_lo_ready, 1)

            def steps(base, ts):
                for t in ts:
                    b, q = base + t, t % 2
                    if t < 2:
                        dve.wait_ge(ot_hi_ready, b + 1)
                        until(dve, o_projected, b - 1)
                        dve.tensor_tensor(ot_lo[:, q], ot_in[:, q], ot_hi[:, q].bitcast(F32), ALU.subtract)\
                           .then_inc(ot_lo_ready, 1)
                        if isinstance(b, int) and b == 0:
                            split_wo()
                    if real(b - 2):
                        dve.wait_ge(xh_ready, b - 1)
                        dve.tensor_tensor(xl_b[:, :, b - 2, :], X2_ps, xh_b[:, :, b - 2, :], ALU.subtract)\
                           .then_inc(xl_ready, 1)
                    if real(b - 1) and t < 3:
                        r, w = b - 1, (t - 1) % 2
                        dve.wait_ge(o_projected, r + 1)
                        dve.wait_ge(xb_ready, r + 1)
                        until(dve, x1_stored[w], 8 * (r - w))
                        dve.tensor_tensor(x1[:, w], O_ps[w], x_again[:, w], ALU.add).then_inc(x1_ready, 1)
                        dve.wait_ge(x1_ready, r + 1)
                        for h in range(2):
                            dve.bn_stats(c_stats[:, h], x1[:, w, h * 512:(h + 1) * 512]).then_inc(c_stats_ready, 1)
                        dve.wait_ge(c_stats_ready, 2 * r + 2)
                        apart(dve, dve_passed)
                        dve.bn_aggr(c_moments[:], c_stats[:].rearrange("p a b -> p (a b)")).then_inc(c_moments_ready, 1)
                        dve.wait_ge(c_moments_ready, r + 1)
                        dve.tensor_scalar(c_var[:], c_moments[:, 1:2], EPS, XS ** -2, ALU.add, ALU.mult)\
                           .then_inc(c_var_ready, 1)
                        dve.wait_ge(c_rstd_ready, r + 1)
                        until(dve, xn2_transposed, r)
                        dve.tensor_scalar(xn2[:, 0], x1[:, w], c_moments[:, 0:1], c_rstd[:, 0:1],
                                          ALU.subtract, ALU.mult).then_inc(xn2_ready, 1)

            pairs_of_batches(dve, steps, 2)

        @block.tensor
        def _(pe):
            def steps(base, ts):
                for t in ts:
                    b, q = base + t, t % 2
                    if t < 2:
                        pe.wait_ge(ot_lo_ready, b + 1)
                        until(pe, x1_ready, b - 1)
                        for j in range(KT):
                            if isinstance(b, int) and b == 0:
                                pe.wait_ge(wo_lo_ready, j + 1)
                            for part, weights in ((ot_hi, (wo_hi, wo_lo)), (ot_lo, (wo_hi,))):
                                for w in weights:
                                    for h in range(2):
                                        mm = pe.matmul(O_ps[q][:, h * 512:(h + 1) * 512],
                                                       part[:, q, j * P:(j + 1) * P], w[:, j, h * 512:(h + 1) * 512],
                                                       start=(j == 0 and part is ot_hi and w is wo_hi),
                                                       stop=(j == KT - 1 and part is ot_lo))
                        mm.then_inc(o_projected, 1)
                    if real(b - 1):
                        pe.wait_ge(xn2_ready, b)
                        until(pe, xl_ready, b - 1)
                        for k in range(KT):
                            mm = pe.transpose(X2_ps[:, k], xn2[:, 0, k * P:(k + 1) * P], ident[:])
                        mm.then_inc(xn2_transposed, 1)

            pairs_of_batches(pe, steps, 1)

        c_block.close()

        d_block = ExitStack()
        block = d_block.enter_context(nc.Block())
        G_ps, U_ps = banks[0], banks[1]
        D_ps = [banks[2][:, 0], banks[2][:, 1], banks[3][:, 0], banks[3][:, 1]]
        UPC = FB
        DPC = 2 * TPC
        SPB = NCH
        LAST = NBLK - 2

        def column(table, n):
            return table[:, n:n + 1] if isinstance(n, int) else table[:, bass.ds(n, 1)]

        def pairs_of_blocks(eng, steps):
            steps(0, 0)
            with eng.Fori(1, NBLK // 2 - 1) as i:
                steps(i * 2 * SPB, i * 2)
            steps(LAST * SPB, LAST)

        @block.sync
        def _(sp):
            sp.dma_start(ds_rows[:], down_s.partition_broadcast(P)).then_inc(scales_loaded, 16)

            for f in range(2):
                sp.dma_start(d_raw[:, f], down_w[f]).then_inc(d_loaded[f], 16)

            def load_gu(a, kind, tile, q):
                until(sp, gu_ready, a - 1)
                sp.dma_start(gu_raw[:, q], (gate_w, up_w)[kind][tile].rearrange("p k f -> p (k f)"))\
                  .then_inc(gu_loaded[q], 16)

            def load_d(a, tile, q):
                until(sp, d_ready, a - 1)
                sp.dma_start(d_raw[:, q], down_w[tile]).then_inc(d_loaded[q], 16)

            def steps(base, block0):
                for n in range(2):
                    nxt = block0 + n + 1
                    if isinstance(nxt, int) and nxt >= NBLK:
                        continue
                    for c in range(4):
                        load_gu(nxt * 4 + c, c // 2, nxt * 2 + c % 2, c % 2)
                        if c % 2:
                            load_d(nxt * 2 + c // 2, nxt * 2 + c // 2, c // 2)

            pairs_of_blocks(sp, steps)
            sp.wait_ge(gu_ready, 4 * NBLK)
            for tile in range(NB + 2):
                if tile < NB:
                    until(sp, y_ready, 2 * (tile - 1))
                    sp.dma_start(x1_in[:, tile % 2], x1_scratch[tile]).then_inc(x1_loaded[tile % 2], 16)
                if tile >= 2:
                    sp.wait_ge(y_ready, 2 * (tile - 1))
                    sp.dma_start(out[tile - 2], acc[:, tile - 2]).then_inc(y_stored, 16)
            sp.wait_ge(y_stored, 16 * NB)

        @block.gpsimd
        def _(pool):
            def steps(base, block0):
                for t in range(2 * SPB):
                    r = base + t
                    for f in range(FB):
                        u = r * UPC + f
                        pool.wait_ge(h_hi_ready, u + 1)
                        until(pool, downed, (r - 1) * DPC)
                        pool.tensor_tensor(h_lo[:, t % 2, f], h_f[:, f % 2], h_hi[:, t % 2, f].bitcast(F32),
                                           ALU.subtract).then_inc(h_lo_ready, 1)
                    if isinstance(r, int) and r > LAST * SPB + SPB:
                        scale(t - SPB - 1)
                if isinstance(base, int) and base > 0:
                    scale(SPB - 1)

            def scale(c):
                for v in range(DPC):
                    tile, h = c * TPC + v // 2, slice(v % 2 * 512, v % 2 * 512 + 512)
                    pool.wait_ge(acc_added, ((NBLK - 1) * SPB + c) * DPC + v + 1)
                    pool.tensor_tensor(acc[:, tile, h], acc[:, tile, h], ds_rows[:, h], ALU.mult).then_inc(acc_scaled, 1)

            pool.wait_ge(scales_loaded, 48)
            pairs_of_blocks(pool, steps)

        @block.scalar
        def _(act):
            def convert(a, c, buf, before):
                act.wait_ge(gu_loaded[c % 2], 8 * (a - c % 2) + 16)
                until(act, upped, before)
                act.activation(gu_w[buf][:, c // 2, c % 2].rearrange("p k f -> p (k f)"), gu_raw[:, c % 2],
                               ACT.Copy).then_inc(gu_ready, 1)

            act.wait_ge(scales_ready, 2)

            def steps(base, block0):
                for t in range(2 * SPB):
                    r, n, c = base + t, block0 + t // SPB, t % SPB
                    for f in range(FB):
                        u = r * UPC + f
                        act.wait_ge(gated, u + 1)
                        until(act, h_ready, u - 1)
                        apart(act, act_passed)
                        act.activation(silu[:, f % 2], G_ps[:, f % 2], ACT.Silu,
                                       scale=column(g_sx, n * FB + f)).then_inc(silu_ready, 1)
                        act.wait_ge(h_ready, u + 1)
                        until(act, downed, (r - 1) * DPC)
                        act.activation(h_hi[:, t % 2, f], h_f[:, f % 2], ACT.Copy).then_inc(h_hi_ready, 1)
                    if not (isinstance(n, int) and n + 1 >= NBLK):
                        convert((n + 1) * 4 + c, c, (t // SPB + 1) % 2, n * SPB * UPC)

            pairs_of_blocks(act, steps)

        @block.vector
        def _(dve):
            dve.wait_ge(scales_loaded, 48)
            dve.tensor_scalar(g_sx[:], g_s[:], 1 / XS, None, ALU.mult).then_inc(scales_ready, 1)
            dve.tensor_scalar(u_sx[:], u_s[:], 1 / XS, None, ALU.mult).then_inc(scales_ready, 1)

            def convert(a, f, buf, before):
                dve.wait_ge(d_loaded[f], 8 * (a - f) + 16)
                until(dve, downed, before)
                dve.tensor_copy(d_w[:, buf, f], d_raw[:, f]).then_inc(d_ready, 1)

            for f in range(FB):
                convert(f, f, 0, 0)
            dve.wait_ge(scales_ready, 2)

            def add(r, c):
                for v in range(DPC):
                    tile, h = c * TPC + v // 2, slice(v % 2 * 512, v % 2 * 512 + 512)
                    dve.wait_ge(downed, r * DPC + v + 1)
                    if isinstance(r, int) and r < SPB:
                        dve.tensor_copy(acc[:, tile, h], D_ps[v % 4]).then_inc(acc_added, 1)
                    else:
                        dve.tensor_tensor(acc[:, tile, h], D_ps[v % 4], acc[:, tile, h], ALU.add)\
                           .then_inc(acc_added, 1)
                    if isinstance(r, int) and r >= (NBLK - 1) * SPB and v >= 2:
                        residual(c, v - 2)
                if isinstance(r, int) and r >= (NBLK - 1) * SPB:
                    residual(c, DPC - 2)
                    residual(c, DPC - 1)

            def residual(c, v):
                tile, h = c * TPC + v // 2, slice(v % 2 * 512, v % 2 * 512 + 512)
                dve.wait_ge(acc_scaled, c * DPC + v + 1)
                dve.wait_ge(x1_loaded[tile % 2], 16 * (tile // 2 + 1))
                dve.tensor_tensor(acc[:, tile, h], acc[:, tile, h], x1_in[:, tile % 2, h], ALU.add).then_inc(y_ready, 1)

            def steps(base, block0):
                for t in range(2 * SPB):
                    r, n, c = base + t, block0 + t // SPB, t % SPB
                    for f in range(FB):
                        u = r * UPC + f
                        dve.wait_ge(upped, u + 1)
                        dve.wait_ge(silu_ready, u + 1)
                        until(dve, h_lo_ready, u - 1)
                        dve.scalar_tensor_tensor(out=h_f[:, f % 2], in0=U_ps[:, f % 2], scalar=column(u_sx, n * FB + f),
                                                 in1=silu[:, f % 2], op0=ALU.mult, op1=ALU.mult).then_inc(h_ready, 1)
                    if real(r - 1):
                        add(r - 1, (t - 1) % SPB)
                    if c % 2 and not (isinstance(n, int) and n + 1 >= NBLK):
                        convert((n + 1) * 2 + c // 2, c // 2, (t // SPB + 1) % 2, n * SPB * DPC)
                if isinstance(base, int) and base > 0:
                    add(base + 2 * SPB - 1, SPB - 1)

            pairs_of_blocks(dve, steps)

        @block.tensor
        def _(pe):
            def down(r, c, buf, slot):
                pe.wait_ge(h_lo_ready, r * UPC + UPC)
                for v in range(DPC):
                    until(pe, acc_added, r * DPC + v - 3)
                    for f in range(FB):
                        for part in (h_hi, h_lo):
                            mm = pe.matmul(D_ps[v % 4], part[:, slot, f, v // 2 * P:(v // 2 + 1) * P],
                                           d_w[:, buf, f, v % 2 * 512:v % 2 * 512 + 512],
                                           start=(f == 0 and part is h_hi), stop=(f == FB - 1 and part is h_lo))
                    mm.then_inc(downed, 1)

            def steps(base, block0):
                for t in range(2 * SPB):
                    r, n, c, buf = base + t, block0 + t // SPB, t % SPB, t // SPB
                    if c == 0:
                        pe.wait_ge(gu_ready, n * 4 + 4)
                    tokens = slice(c * CH, (c + 1) * CH)
                    for f in range(FB):
                        u = r * UPC + f
                        for kind, (bank, done, free) in enumerate(((G_ps, gated, silu_ready), (U_ps, upped, h_ready))):
                            until(pe, free, u - 1)
                            for k in range(KT):
                                for part in (xh, xl):
                                    mm = pe.matmul(bank[:, f % 2], gu_w[buf][:, kind, f, k], part[:, k, tokens],
                                                   start=(k == 0 and part is xh), stop=(k == KT - 1 and part is xl))
                            mm.then_inc(done, 1)
                    if real(r - 1):
                        if c == 1:
                            pe.wait_ge(d_ready, n * 2 + 2)
                        down(r - 1, (c - 1) % SPB, (t - 1) // SPB % 2, (t - 1) % 2)
                if isinstance(base, int) and base > 0:
                    down(base + 2 * SPB - 1, SPB - 1, 1, 1)

            pairs_of_blocks(pe, steps)

        d_block.close()


def kernel(**inputs):
    import numpy as np
    import concourse.bacc as bacc
    from concourse.bass_utils import run_bass_kernel_spmd

    a = {n: np.asarray(v) for n, v in inputs.items()}

    def tiled(w):
        return w.reshape(-1, P, w.shape[1])

    def transposed_tiles(w):
        return w.reshape(FT, P, KT, P).transpose(0, 3, 2, 1)

    row = np.arange(P)
    pair_d = row // STATES
    arrays = {
        "x": a["x"],
        "ctx_t": a["ctx_4096"].reshape(NB, P, KT, P).transpose(0, 3, 2, 1),
        "wqkv": np.stack([tiled(a[f"L0_xattn_W{c}"]) for c in "qkv"], 1).reshape(3 * KT, P, D),
        "b_qk": np.stack([a["L0_xattn_bq"], a["L0_xattn_bk"]], -1).reshape(KT, P, 2).transpose(1, 0, 2),
        "b_v": a["L0_xattn_bv"].reshape(KT, P).T,
        "mix_rows": np.repeat(a["L0_xattn_interference"][:, None], DK, 1).reshape(KT, P, STATES).transpose(1, 0, 2),
        "amp": a["L0_xattn_amp"],
        "wo_t": a["L0_xattn_Wo"].T.reshape(HEADS, DK, STATES, D).transpose(0, 2, 1, 3).reshape(KT, P, D),
        "b_o": a["L0_xattn_bo"],
        "gate_w": transposed_tiles(a["L0_ffn_gate_wq"]),
        "gate_s": a["L0_ffn_gate_scale"].reshape(FT, P).T,
        "up_w": transposed_tiles(a["L0_ffn_up_wq"]),
        "up_s": a["L0_ffn_up_scale"].reshape(FT, P).T,
        "down_w": a["L0_ffn_down_wq"].T.reshape(FT, P, D),
        "down_s": a["L0_ffn_down_scale"],
        "ident_c": np.eye(P, dtype=np.float32),
        "pair_mask_c": (row[:, None] // DK == np.arange(PAIRS)).astype(np.float32),
        "fold_mask_c": (pair_d[:, None] == np.arange(HT * DK)).astype(np.float32).reshape(P, HT, DK),
        "state_eye_c": (row[:, None] % STATES == np.arange(STATES)).astype(np.float32),
    }
    nc = bacc.Bacc("TRN2", target_bir_lowering=False, num_devices=1)
    arrays = {n: np.ascontiguousarray(v) for n, v in arrays.items()}
    handles = {n: nc.dram_tensor(n, v.shape, mybir.dt.from_np(v.dtype), kind="ExternalInput").ap()
               for n, v in arrays.items()}
    out = nc.dram_tensor("out", (NB, P, D), F32, kind="ExternalOutput").ap()
    program(nc, out=out, **handles)
    result = run_bass_kernel_spmd(nc, [arrays], core_ids=[0])
    return result.results[0]["out"]
```

```python
from contextlib import ExitStack

import concourse.bass as bass
from concourse import mybir

F32 = mybir.dt.float32
F32R = mybir.dt.float32r
F16 = mybir.dt.float16
BF16 = mybir.dt.bfloat16
I32 = mybir.dt.int32
ALU = mybir.AluOpType
ACT = mybir.ActivationFunctionType
AX = mybir.AxisListType.X

P = 128
NB = 16
D = 1024
KT = D // P
HEADS, STATES, DK = 16, 4, 16
PAIRS = P // DK
HT = P // (STATES * DK)
VP = 3 * DK + 1
VS = VP + 1
STEPS = NB * KT
SCALE = DK ** -0.5
E_SHIFT = 9.704060527839234
EPS = 1e-5
HID = 3584
FT = HID // P
FB = 2
NBLK = FT // FB
CH = 512
NCH = NB * P // CH
TPC = CH // P
XS = 256.0
TOP = 2.0 ** 13


def until(eng, sem, value):
    if not isinstance(value, int) or value > 0:
        eng.wait_ge(sem, value)


def apart(eng, passed):
    eng.sem_inc(passed, 1)


def real(step):
    return not (isinstance(step, int) and step < 0)


def program(nc, x, ctx_t, wqkv, b_qk, b_v, mix_rows, amp, wo_t, b_o, gate_w, gate_s, up_w, up_s,
            down_w, down_s, ident_c, pair_mask_c, fold_mask_c, state_eye_c, out):
    ot_scratch = nc.dram_tensor("ot_scratch", (NB, P, KT, P), F32, kind="Internal").ap()
    x1_scratch = nc.dram_tensor("x1_scratch", (NB, P, D), F32, kind="Internal").ap()

    with ExitStack() as ctx:
        def sb(name, shape, dt, scope=ctx):
            return scope.enter_context(nc.sbuf_tensor(name, shape, dt))

        def sem(name):
            return ctx.enter_context(nc.semaphore(name))

        banks = [ctx.enter_context(nc.psum_tensor(f"banks{i}", [P, 2, 512], F32)) for i in range(4)]

        ident = sb("ident", [P, P], F32)
        pair_mask = sb("pair_mask", [P, PAIRS], F32)
        raw = sb("raw", [P, 2 * 3, D], F32)

        b_scope = ExitStack()
        w_hi = sb("w_hi", [P, 3, KT, D], F16, b_scope)
        w_lo = sb("w_lo", [P, 3, KT, D], F16, b_scope)
        w_inv = sb("w_inv", [P, KT, 3], F32, b_scope)
        q_inv = sb("q_inv", [P, KT], F32, b_scope)
        ctx_scale = sb("ctx_scale", [P, 1], F32, b_scope)
        ctx_inv = sb("ctx_inv", [P, 1], F32, b_scope)
        kv_inv = sb("kv_inv", [P, 2, KT, 2], F32, b_scope)
        binade = sb("binade", [P, 2, 3], F32, b_scope)
        ctx_max = sb("ctx_max", [P, 1], F32, b_scope)
        ctx_all_max = sb("ctx_all_max", [P, 1], F32, b_scope)
        bias_qk = sb("bias_qk", [P, KT, 2], F32, b_scope)
        bias_v = sb("bias_v", [P, D], F32, b_scope)
        xn = sb("xn", [P, 2, D], F32, b_scope)
        xn_hi = sb("xn_hi", [P, 2, KT, P], F16, b_scope)
        xn_lo = sb("xn_lo", [P, 2, KT, P], F16, b_scope)
        ctx_raw = sb("ctx_raw", [P, KT, P], F32, b_scope)
        ctx_hi = sb("ctx_hi", [P, 2, KT, P], F16, b_scope)
        ctx_lo = sb("ctx_lo", [P, 2, KT, P], F16, b_scope)
        stats = sb("stats", [P, 2, 6], F32, b_scope)
        moments = sb("moments", [P, 2], F32, b_scope)
        var_eps = sb("var_eps", [P, 1], F32, b_scope)
        minus_half = sb("minus_half", [P, 1], F32, b_scope)
        rstd = sb("rstd", [P, 1], F32, b_scope)
        a_scope = ExitStack()
        w_raw_more = sb("w_raw_more", [P, 3, D], F32, a_scope)
        w_raw = [raw[:, 0:3], raw[:, 3:6], w_raw_more[:]]
        w_s = sb("w_s", [P, 3, 2, D], F32, a_scope)
        w_scale = sb("w_scale", [P, 3, 3], F32, a_scope)
        w_part_max = sb("w_part_max", [P, 3], F32, a_scope)
        w_all_max = sb("w_all_max", [P, 3], F32, a_scope)
        w_bound = sb("w_bound", [P, 3], F32, a_scope)
        fold_part_max = sb("fold_part_max", [P, 1], F32, a_scope)
        fold_all_max = sb("fold_all_max", [P, 1], F32, a_scope)
        fold_growth = sb("fold_growth", [P, 1], F32, a_scope)
        fold = sb("fold", [P, KT * P], F32, a_scope)
        fold_mask = sb("fold_mask", [P, HT, DK], F32, a_scope)
        state_eye = sb("state_eye", [P, STATES], F32, a_scope)
        mix = sb("mix", [P, KT, STATES], F32, a_scope)
        amp_sb = sb("amp_sb", [P, 1], F32, a_scope)
        amp_tenth = sb("amp_tenth", [P, 1], F32, a_scope)
        bqk_raw = sb("bqk_raw", [P, KT, 2], F32, a_scope)
        bv_raw = sb("bv_raw", [P, KT], F32, a_scope)
        bv_wide = sb("bv_wide", [P, KT, P], F32, a_scope)
        a_scope.close()
        qk_f = sb("qk_f", [P, 2, 2, P], F32, b_scope)
        qk_hi = sb("qk_hi", [P, 2, 2, P], F32R, b_scope)
        qk_lo = sb("qk_lo", [P, 2, 2, P], F32R, b_scope)
        k_wide_hi = sb("k_wide_hi", [P, 2, PAIRS, P], F32R, b_scope)
        k_wide_lo = sb("k_wide_lo", [P, 2, PAIRS, P], F32R, b_scope)
        v_f = sb("v_f", [P, 2, P], F32, b_scope)
        v_rest = sb("v_rest", [P, 2, P], F32, b_scope)
        v_parts = sb("v_parts", [P, 4, PAIRS, VS], BF16, b_scope)
        neg_max = sb("neg_max", [P, 2, PAIRS], F32, b_scope)
        s_m = sb("s_m", [P, 2, PAIRS, P], F32, b_scope)
        e_f = sb("e_f", [P, 2, PAIRS, P], F32, b_scope)
        e_hi = sb("e_hi", [P, 2, PAIRS, P], F16, b_scope)
        e_lo = sb("e_lo", [P, 2, PAIRS, P], F16, b_scope)
        o_sum = sb("o_sum", [P, 2, PAIRS, DK], F32, b_scope)
        r_den = sb("r_den", [P, 2, PAIRS, 1], F32, b_scope)
        o_tok = sb("o_tok", [P, 2, P], F32, b_scope)
        o_t = sb("o_t", [P, 2, P], F32, b_scope)
        b_scope.close()

        wo_scope = ExitStack()
        wo_hi = sb("wo_hi", [P, KT, D], F32R, wo_scope)
        wo_lo = sb("wo_lo", [P, KT, D], F32R, wo_scope)
        wo_scope.close()
        acc = sb("acc", [P, NB, D], F32)
        h_hi = sb("h_hi", [P, 2, FB, CH], F32R)
        h_lo = sb("h_lo", [P, 2, FB, CH], F32R)
        ot_hi, ot_lo = h_hi[:].rearrange("p a f t -> p a (f t)"), h_lo[:].rearrange("p a f t -> p a (f t)")
        xh = sb("xh", [P, KT, NB * P], F16)
        xl = sb("xl", [P, KT, NB * P], F16)
        gu_w = [sb("gu_w0", [P, 2, FB, KT, P], F16)]
        g_s = sb("g_s", [P, FT], F32)
        u_s = sb("u_s", [P, FT], F32)
        g_sx = sb("g_sx", [P, FT], F32)
        u_sx = sb("u_sx", [P, FT], F32)
        c_scope = ExitStack()
        wo_raw, ot_in = raw[:, 0:4], raw[:, 4:6]
        bo_rows = sb("bo_rows", [P, D], F32, c_scope)
        x_again = sb("x_again", [P, 2, D], F32, c_scope)
        x1 = sb("x1", [P, 2, D], F32, c_scope)
        xn2 = sb("xn2", [P, 1, D], F32, c_scope)
        c_stats = sb("c_stats", [P, 2, 6], F32, c_scope)
        c_moments = sb("c_moments", [P, 2], F32, c_scope)
        c_var = sb("c_var", [P, 1], F32, c_scope)
        c_half = sb("c_half", [P, 1], F32, c_scope)
        c_rstd = sb("c_rstd", [P, 1], F32, c_scope)
        c_scope.close()

        d_scope = ExitStack()
        gu_raw, d_raw = raw[:, 0:2].bitcast(I32), raw[:, 2:4].bitcast(I32)
        gu_w.append(sb("gu_w1", [P, 2, FB, KT, P], F16, d_scope))
        d_w = sb("d_w", [P, 2, FB, D], F32R, d_scope)
        ds_rows = raw[:, 4]
        silu = raw[:, 5].rearrange("p (f t) -> p f t", t=CH)
        h_f = sb("h_f", [P, 2, CH], F32, d_scope)
        x1_in = raw[:, 0:4]
        d_scope.close()

        act_passed, dve_passed, pool_passed = sem("act_passed"), sem("dve_passed"), sem("pool_passed")
        pe_passed = sem("pe_passed")
        fold_parts_loaded, const_loaded = sem("fold_parts_loaded"), sem("const_loaded")
        fold_max_ready, fold_all_max_ready = sem("fold_max_ready"), sem("fold_all_max_ready")
        w_loaded = [sem(f"w_loaded{i}") for i in range(9)]
        amp_ready, mix_ready, fold_ready = sem("amp_ready"), sem("mix_ready"), sem("fold_ready")
        bv_wide_ready = sem("bv_wide_ready")
        bias_made, bias_ready = sem("bias_made"), sem("bias_ready")
        w_folded, w_max_ready, w_all_max_ready = sem("w_folded"), sem("w_max_ready"), sem("w_all_max_ready")
        w_chain, w_hi_ready, w_s_ready = sem("w_chain"), sem("w_hi_ready"), sem("w_s_ready")
        wq_lo_ready, wkv_lo_ready, q_inv_ready = sem("wq_lo_ready"), sem("wkv_lo_ready"), sem("q_inv_ready")
        ctx_max_ready, ctx_all_max_ready = sem("ctx_max_ready"), sem("ctx_all_max_ready")
        ctx_chain, ctx_hi_ready, ctx_lo_ready = sem("ctx_chain"), sem("ctx_hi_ready"), sem("ctx_lo_ready")
        x_loaded = [sem("x_loaded0"), sem("x_loaded1")]
        ctx_loaded = sem("ctx_loaded")
        half_ready = sem("half_ready")
        stats_ready, moments_ready = sem("stats_ready"), sem("moments_ready")
        var_ready, rstd_ready, xn_ready = sem("var_ready"), sem("rstd_ready"), sem("xn_ready")
        xn_transposed, xn_hi_ready, xn_lo_ready = sem("xn_transposed"), sem("xn_hi_ready"), sem("xn_lo_ready")
        projected = sem("projected")
        qk_kept, qk_hi_ready, qk_lo_ready = sem("qk_kept"), sem("qk_hi_ready"), sem("qk_lo_ready")
        k_wide_hi_ready, k_wide_lo_ready, v_kept = sem("k_wide_hi_ready"), sem("k_wide_lo_ready"), sem("v_kept")
        ones_ready, v_chain, v_split = sem("ones_ready"), sem("v_chain"), sem("v_split")
        scored, max_ready, sm_ready = sem("scored"), sem("max_ready"), sem("sm_ready")
        s_transposed, e_hi_ready, e_ready = sem("s_transposed"), sem("e_hi_ready"), sem("e_ready")
        e_lo_ready, attended = sem("e_lo_ready"), sem("attended")
        o_summed, den_ready, o_ready = sem("o_summed"), sem("den_ready"), sem("o_ready")
        o_transposed, o_t_kept = sem("o_transposed"), sem("o_t_kept")
        o_t_stored = [sem("o_t_stored0"), sem("o_t_stored1")]

        bo_loaded, wo_loaded = sem("bo_loaded"), [sem(f"wo_loaded{i}") for i in range(4)]
        wo_hi_ready, wo_lo_ready = sem("wo_hi_ready"), sem("wo_lo_ready")
        ot_loaded, xa_loaded = [sem("ot_loaded0"), sem("ot_loaded1")], [sem("xa_loaded0"), sem("xa_loaded1")]
        ot_hi_ready, ot_lo_ready, xb_ready = sem("ot_hi_ready"), sem("ot_lo_ready"), sem("xb_ready")
        o_projected, x1_ready = sem("o_projected"), sem("x1_ready")
        x1_stored = [sem("x1_stored0"), sem("x1_stored1")]
        c_half_ready, c_stats_ready, c_moments_ready = sem("c_half_ready"), sem("c_stats_ready"), sem("c_moments_ready")
        c_var_ready, c_rstd_ready, xn2_ready = sem("c_var_ready"), sem("c_rstd_ready"), sem("xn2_ready")
        xn2_transposed, xh_ready, xl_ready = sem("xn2_transposed"), sem("xh_ready"), sem("xl_ready")
        scales_loaded, scales_ready = sem("scales_loaded"), sem("scales_ready")
        gu_loaded, d_loaded = [sem("gu_loaded0"), sem("gu_loaded1")], [sem("d_loaded0"), sem("d_loaded1")]
        gu_ready, d_ready = sem("gu_ready"), sem("d_ready")
        gated, upped, silu_ready = sem("gated"), sem("upped"), sem("silu_ready")
        h_ready, h_hi_ready, h_lo_ready = sem("h_ready"), sem("h_hi_ready"), sem("h_lo_ready")
        downed, acc_added, acc_scaled = sem("downed"), sem("acc_added"), sem("acc_scaled")
        x1_loaded, y_ready, y_stored = [sem(f"x1_loaded{i}") for i in range(4)], sem("y_ready"), sem("y_stored")

        S_ps, T_ps, QKV_ps = banks[0], banks[1], banks[2]
        PV_ps = banks[3][:, 0, :]
        XT_ps = banks[3][:, 1, 0:P]
        OT_ps = banks[3][:, 1, P:2 * P]
        X0_ps = banks[3][:].rearrange("p b n -> p (b n)")
        O_ps = [b[:].rearrange("p b n -> p (b n)") for b in banks[2:4]]
        G_ps, U_ps = banks[0], banks[1]
        S_flat = S_ps[:].rearrange("p b n -> p (b n)")
        T_flat = T_ps[:].rearrange("p b n -> p (b n)")
        S_pairs = S_flat.rearrange("p (c k) -> p c k", c=PAIRS)
        T_pairs = T_flat.rearrange("p (c k) -> p c k", c=PAIRS)
        PV_pairs = PV_ps[:, 0:PAIRS * VP].rearrange("p (c n) -> p c n", n=VP)

        W_ps = (S_pairs, T_pairs, QKV_ps[:].rearrange("p b (c k) -> p (b c) k", k=P))

        def other_tiles(eng, tiles):
            with eng.Fori(0, (KT - 2) // 3) as i:
                for g in range(3):
                    tiles(3 * i + 2 + g, (2 + g) % 3, i + (2 if g else 1))

        w_s_tiles = w_s[:].rearrange("p g m (k f) -> p g m k f", f=P)
        w_inv_flat = w_inv[:].rearrange("p j m -> p (j m)")

        def at3(j):
            return slice(3 * j, 3 * j + 3) if isinstance(j, int) else bass.ds(3 * j, 3)

        def at(j):
            return slice(j * P, j * P + P) if isinstance(j, int) else bass.ds(j * P, P)

        def split_wo(eng, tiles):
            for j in tiles:
                if eng is nc.scalar:
                    eng.wait_ge(wo_loaded[j % 4], 16 * (j // 4 + 1))
                    eng.activation(wo_hi[:, j], wo_raw[:, j % 4], ACT.Copy).then_inc(wo_hi_ready, 1)
                else:
                    eng.wait_ge(wo_hi_ready, j + 1)
                    eng.tensor_tensor(wo_lo[:, j], wo_raw[:, j % 4], wo_hi[:, j].bitcast(F32), ALU.subtract)\
                       .then_inc(wo_lo_ready, 1)

        def split_ot(eng, n):
            if eng is nc.scalar:
                eng.wait_ge(ot_loaded[n], 16)
                eng.activation(ot_hi[:, n], ot_in[:, n], ACT.Copy).then_inc(ot_hi_ready, 1)
            else:
                eng.wait_ge(ot_hi_ready, n + 1)
                eng.tensor_tensor(ot_lo[:, n], ot_in[:, n], ot_hi[:, n].bitcast(F32), ALU.subtract)\
                   .then_inc(ot_lo_ready, 1)

        def project_out(pe, q, j):
            for part, weights in ((ot_hi, (wo_hi, wo_lo)), (ot_lo, (wo_hi,))):
                for w in weights:
                    for h in range(2):
                        mm = pe.matmul(O_ps[q][:, h * 512:(h + 1) * 512],
                                       part[:, q, j * P:(j + 1) * P], w[:, j, h * 512:(h + 1) * 512],
                                       start=(j == 0 and part is ot_hi and w is wo_hi),
                                       stop=(j == KT - 1 and part is ot_lo))
            return mm

        def up_or_gate(pe, bank, kind, f, buf, tokens):
            for k in range(KT):
                for part in (xh, xl):
                    mm = pe.matmul(bank[:, f % 2], gu_w[buf][:, kind, f, k], part[:, k, tokens],
                                   start=(k == 0 and part is xh), stop=(k == KT - 1 and part is xl))
            return mm

        ab_scope = ExitStack()
        block = ab_scope.enter_context(nc.Block())

        @block.sync
        def _(sp):
            small = [(mix[:], mix_rows), (amp_sb[:], amp.partition_broadcast(P)), (state_eye[:], state_eye_c),
                     (fold_mask[:], fold_mask_c), (ident[:], ident_c), (bqk_raw[:], b_qk), (bv_raw[:], b_v),
                     (pair_mask[:], pair_mask_c)]
            for n, (dst, src) in enumerate(small):
                sp.dma_start(dst, src).then_inc(fold_parts_loaded if n < 4 else const_loaded, 16)
            for c in range(3):
                sp.dma_start(w_raw[0][:, c], wqkv[c]).then_inc(w_loaded[c], 16)
            sp.dma_start(xn[:, 0], x[0]).then_inc(x_loaded[0], 16)
            for c in range(3, 9):
                if c == 6:
                    sp.dma_start(ctx_raw[:], ctx_t[0]).then_inc(ctx_loaded, 16)
                sp.dma_start(w_raw[c // 3][:, c % 3], wqkv[c]).then_inc(w_loaded[c], 16)
            sp.dma_start(xn[:, 1], x[1]).then_inc(x_loaded[1], 16)
            for n in range(9, 3 * KT):
                sp.wait_ge(w_folded, n - 8)
                sp.wait_ge(w_max_ready, n // 3 - 2)
                sp.dma_start(w_raw[n // 3 % 3][:, n % 3], wqkv[n]).then_inc(w_loaded[n % 9], 16)
            sp.wait_ge(ctx_lo_ready, 1)
            sp.dma_start(ctx_raw[:], ctx_t[1]).then_inc(ctx_loaded, 16)

            def steps(base, batch, ts):
                for t in ts:
                    b, j = batch + t // KT, t % KT
                    if j == 0 and t < 16 and not (isinstance(b, int) and b + 2 >= NB):
                        sp.wait_ge(xn_transposed, KT * b + KT)
                        sp.dma_start(xn[:, t // KT], x[b + 2]).then_inc(x_loaded[t // KT], 16)
                    if j == 5 and t < 16 and not (isinstance(b, int) and b + 2 >= NB):
                        sp.wait_ge(ctx_lo_ready, b + 2)
                        sp.dma_start(ctx_raw[:], ctx_t[b + 2]).then_inc(ctx_loaded, 16)
                    if isinstance(b, int) and t == 8 and b == NB - 1:
                        for c in range(4):
                            sp.dma_start(wo_raw[:, c], wo_t[c]).then_inc(wo_loaded[c], 16)
                        for n in range(2):
                            sp.dma_start(ot_in[:, n], ot_scratch[n].rearrange("p k t -> p (k t)"))\
                              .then_inc(ot_loaded[n], 16)
                    r, w = base + t - 5, (t - 5) % 2
                    if isinstance(r, int) and r < 0:
                        continue
                    rb, rj = batch + (t - 5) // KT, (t - 5) % KT
                    sp.wait_ge(o_t_kept, r + 1)
                    sp.dma_start(ot_scratch[rb, :, rj, :], o_t[:, w]).then_inc(o_t_stored[w], 16)
                    if t == 16:
                        for c in range(4, KT):
                            sp.wait_ge(wo_lo_ready, c - 3)
                            sp.dma_start(wo_raw[:, c % 4], wo_t[c]).then_inc(wo_loaded[c % 4], 16)

            steps(0, 0, range(16))
            with sp.Fori(1, NB // 2 - 1) as i:
                steps(i * 16, i * 2, range(16))
            steps(STEPS - 16, NB - 2, range(16))
            steps(STEPS - 16, NB - 2, range(16, 21))
            for q in o_t_stored:
                sp.wait_ge(q, 16 * STEPS // 2)

        @block.gpsimd
        def _(pool):
            pool.memset(minus_half[:], -0.5).then_inc(half_ready, 1)
            pool.wait_ge(half_ready, 1)

            def root(n):
                pool.wait_ge(var_ready, n + 1)
                pool.tensor_tensor(rstd[:], var_eps[:], minus_half[:], ALU.pow).then_inc(rstd_ready, 1)

            def ctx_maximum(n):
                pool.wait_ge(ctx_max_ready, n + 1)
                apart(pool, pool_passed)
                pool.partition_all_reduce(ctx_all_max[:], ctx_max[:], P, bass.bass_isa.ReduceOp.max)\
                    .then_inc(ctx_all_max_ready, 1)

            def reduce_max(j):
                pool.wait_ge(w_max_ready, j + 1)
                until(pool, w_chain, 6 * j)
                apart(pool, pool_passed)
                pool.partition_all_reduce(w_all_max[:], w_part_max[:], P, bass.bass_isa.ReduceOp.max)\
                    .then_inc(w_all_max_ready, 1)

            def tiles(j, g, load):
                reduce_max(j)
                lows(j - 1, (g + 2) % 3)

            def lows(j, g):
                for m in range(2):
                    pool.wait_ge(w_s_ready, 2 * j + m + 1)
                    apart(pool, pool_passed)
                    pool.tensor_tensor(w_lo[:, 1 + m, :, at(j)], w_s_tiles[:, g, m], w_hi[:, 1 + m, :, at(j)],
                                       ALU.subtract).then_inc(wkv_lo_ready, 1)

            pool.wait_ge(fold_max_ready, 1)
            pool.partition_all_reduce(fold_all_max[:], fold_part_max[:], P, bass.bass_isa.ReduceOp.max)\
                .then_inc(fold_all_max_ready, 1)
            reduce_max(0)
            root(0)
            reduce_max(1)
            ctx_maximum(0)
            lows(0, 0)
            other_tiles(pool, tiles)
            root(1)
            lows(KT - 1, (KT - 1) % 3)
            pool.wait_ge(w_folded, 3 * KT)
            pool.wait_ge(wkv_lo_ready, 2 * KT + 2)
            pool.wait_ge(wq_lo_ready, KT)
            pool.wait_ge(bias_made, 1)
            pool.memset(v_parts[:, :, :, VP - 1:VP], 1.0).then_inc(ones_ready, 1)

            def steps(base, batch, ts):
                for t in ts:
                    s, b, j = base + t, batch + t // KT, t % KT
                    if t < 16:
                        pool.wait_ge(qk_lo_ready, s + 1)
                        until(pool, scored, s - 1)
                        pool.tensor_tensor(k_wide_lo[:, t % 2],
                                           qk_lo[:, t % 2, 1].bitcast(F32).unsqueeze(1).to_broadcast([P, PAIRS, P]),
                                           pair_mask[:].unsqueeze(2).to_broadcast([P, PAIRS, P]), ALU.mult)\
                            .then_inc(k_wide_lo_ready, 1)
                        pool.wait_ge(v_kept, s + 1)
                        until(pool, attended, s - 3)
                        part = [v_parts[:, t % 4, :, DK * q:DK * (q + 1)] for q in range(3)]
                        whole = v_f[:, t % 2].rearrange("p (c d) -> p c d", d=DK)
                        apart(pool, pool_passed)
                        rest = v_rest[:, t % 2].rearrange("p (c d) -> p c d", d=DK)
                        pool.tensor_copy(part[0], whole).then_inc(v_chain, 1)
                        pool.wait_ge(v_chain, 3 * s + 1)
                        pool.tensor_tensor(rest, whole, part[0], ALU.subtract).then_inc(v_chain, 1)
                        pool.wait_ge(v_chain, 3 * s + 2)
                        apart(pool, pool_passed)
                        pool.tensor_copy(part[1], rest).then_inc(v_chain, 1)
                        pool.wait_ge(v_chain, 3 * s + 3)
                        pool.tensor_tensor(part[2], rest, part[1], ALU.subtract).then_inc(v_split, 1)
                    r = s - 2
                    if not (isinstance(r, int) and r < 0) and t < 18:
                        pool.wait_ge(e_ready, r + 1)
                        pool.wait_ge(e_hi_ready, r + 1)
                        until(pool, attended, r - 1)
                        pool.tensor_tensor(e_lo[:, t % 2], e_f[:, t % 2], e_hi[:, t % 2],
                                           ALU.subtract).then_inc(e_lo_ready, 1)
                    if j == 1 and t < 16 and not (isinstance(b, int) and b + 1 >= NB):
                        ctx_maximum(b + 1)
                    if j == 5 and t < 16 and not (isinstance(b, int) and b + 2 >= NB):
                        root(b + 2)

            steps(0, 0, range(16))
            with pool.Fori(1, NB // 2 - 1) as i:
                steps(i * 16, i * 2, range(16))
            steps(STEPS - 16, NB - 2, range(18))

        @block.scalar
        def _(act):
            act.sem_inc(wkv_lo_ready, 2)
            def tiles(j, g, load=1):
                act.wait_ge(w_chain, 6 * j + 6)
                for m in range(3):
                    act.wait_ge(w_folded, 3 * j + m + 1)
                    apart(act, act_passed)
                    act.activation(w_hi[:, m, :, at(j)], W_ps[m], ACT.Copy, scale=w_scale[:, g, m:m + 1])\
                       .then_inc(w_hi_ready, 1)
                    if m > 0:
                        if not isinstance(j, int):
                            act.wait_ge(wkv_lo_ready, 2 * (j - 2) + m)
                        act.activation(w_s_tiles[:, g, m - 1], W_ps[m], ACT.Copy, scale=w_scale[:, g, m:m + 1])\
                           .then_inc(w_s_ready, 1)

            def keep_xn(n, slot, j, before):
                act.wait_ge(xn_transposed, n + 1)
                if j == 0:
                    until(act, projected, before)
                act.activation(xn_hi[:, slot, j], XT_ps, ACT.Copy).then_inc(xn_hi_ready, 1)

            def keep_ctx(n, slot, before):
                act.wait_ge(ctx_chain, 6 * n + 5)
                until(act, projected, before)
                act.activation(ctx_hi[:, slot], ctx_raw[:], ACT.Copy, scale=ctx_scale[:, 0:1])\
                   .then_inc(ctx_hi_ready, 1)

            act.wait_ge(bias_made, 1)
            act.activation(bias_qk[:], QKV_ps[:, 0, 0:2 * KT].rearrange("p (j m) -> p j m", m=2), ACT.Copy)\
               .then_inc(bias_ready, 1)
            act.activation(bias_v[:], X0_ps, ACT.Copy).then_inc(bias_ready, 1)
            tiles(0, 0)
            act.wait_ge(xn_transposed, KT)
            act.activation(xn_hi[:, 0].rearrange("p k t -> p (k t)"), X0_ps, ACT.Copy).then_inc(xn_hi_ready, KT)
            tiles(1, 1)
            keep_ctx(0, 0, 0)
            other_tiles(act, tiles)
            act.wait_ge(ctx_chain, 6)
            act.wait_ge(wq_lo_ready, KT)
            act.wait_ge(wkv_lo_ready, 2 * KT + 2)
            act.wait_ge(q_inv_ready, 1)
            act.wait_ge(bias_ready, 2)

            def steps(base, batch, ts):
                for t in ts:
                    s, b, j = base + t, batch + t // KT, t % KT
                    r = s - 5
                    if not (isinstance(r, int) and r < 0):
                        w = (t - 5) % 2
                        act.wait_ge(o_transposed, r + 1)
                        until(act, o_t_stored[w], 8 * (r - w))
                        act.activation(o_t[:, w], OT_ps, ACT.Copy).then_inc(o_t_kept, 1)
                    if t < 16:
                        act.wait_ge(projected, s + 1)
                        until(act, qk_lo_ready, s - 1)
                        act.activation(qk_f[:, t % 2, 0], QKV_ps[:, t % 2, 0:P], ACT.Identity, scale=q_inv[:, j:j + 1],
                                       bias=bias_qk[:, j, 0:1]).then_inc(qk_kept, 1)
                        act.activation(qk_f[:, t % 2, 1], QKV_ps[:, t % 2, P:2 * P], ACT.Identity,
                                       scale=kv_inv[:, t // KT, j, 0:1], bias=bias_qk[:, j, 1:2]).then_inc(qk_kept, 1)
                        if not (isinstance(b, int) and b + 1 >= NB):
                            keep_xn(s + KT, (t // KT + 1) % 2, j, KT * b)
                        act.wait_ge(qk_kept, 2 * s + 2)
                        until(act, scored, s - 1)
                        act.activation(qk_hi[:, t % 2], qk_f[:, t % 2], ACT.Copy).then_inc(qk_hi_ready, 1)
                        if not (isinstance(b, int) and b + 1 >= NB):
                            if j == 3:
                                keep_ctx(b + 1, (t // KT + 1) % 2, KT * b)
                    if t == 16:
                        act.wait_ge(projected, STEPS)
                        split_ot(act, 0)
                        split_wo(act, range(4))
                    if t == 17:
                        split_wo(act, range(4, 6))
                    r = s - 2
                    if not (isinstance(r, int) and r < 0) and t < 18:
                        act.wait_ge(s_transposed, r + 1)
                        until(act, attended, r - 1)
                        act.activation(e_hi[:, t % 2], T_pairs, ACT.Exp, bias=E_SHIFT, scale=SCALE)\
                           .then_inc(e_hi_ready, 1)
                        until(act, e_lo_ready, r - 1)
                        act.activation(e_f[:, t % 2], T_pairs, ACT.Exp, bias=E_SHIFT, scale=SCALE)\
                           .then_inc(e_ready, 1)
                    if t == 17:
                        split_wo(act, range(6, KT))
                        split_ot(act, 1)

            steps(0, 0, range(16))
            with act.Fori(1, NB // 2 - 1) as i:
                steps(i * 16, i * 2, range(16))
            steps(STEPS - 16, NB - 2, range(21))

        @block.vector
        def _(dve):
            dve.wait_ge(fold_parts_loaded, 16 * 4)
            dve.tensor_scalar(amp_tenth[:], amp_sb[:], 0.1, None, ALU.mult).then_inc(amp_ready, 1)
            dve.wait_ge(amp_ready, 1)
            dve.scalar_tensor_tensor(out=mix[:], in0=mix[:], scalar=amp_tenth[:, 0:1],
                                     in1=state_eye[:].unsqueeze(1).to_broadcast([P, KT, STATES]),
                                     op0=ALU.mult, op1=ALU.add).then_inc(mix_ready, 1)
            dve.wait_ge(mix_ready, 1)
            for j in range(KT):
                dve.tensor_tensor(
                    fold[:, at(j)].rearrange("p (h m d) -> p h m d", h=HT, d=DK),
                    mix[:, j].unsqueeze(1).unsqueeze(3).to_broadcast([P, HT, STATES, DK]),
                    fold_mask[:].unsqueeze(2).to_broadcast([P, HT, STATES, DK]), ALU.mult).then_inc(fold_ready, 1)
            dve.tensor_reduce(fold_part_max[:], mix[:].rearrange("p k m -> p (k m)"), AX, ALU.max,
                              apply_absolute_value=True).then_inc(fold_max_ready, 1)
            dve.wait_ge(const_loaded, 16 * 4)
            dve.tensor_tensor(bv_wide[:], bv_raw[:].unsqueeze(2).to_broadcast([P, KT, P]),
                              ident[:, 0:1].unsqueeze(1).to_broadcast([P, KT, P]), ALU.bypass)\
               .then_inc(bv_wide_ready, 1)
            dve.wait_ge(fold_all_max_ready, 1)
            dve.tensor_scalar(fold_growth[:], fold_all_max[:], float(STATES), None, ALU.mult).then_inc(amp_ready, 1)
            dve.wait_ge(amp_ready, 2)

            def moments_of(n, slot):
                if isinstance(n, int):
                    dve.wait_ge(x_loaded[slot], 16 * (n // 2 + 1))
                else:
                    dve.wait_ge(x_loaded[slot], 8 * (n - slot + 2))
                for q in range(2):
                    dve.bn_stats(stats[:, q], xn[:, slot, q * 512:(q + 1) * 512]).then_inc(stats_ready, 1)
                dve.wait_ge(stats_ready, 2 * n + 2)
                apart(dve, dve_passed)
                dve.bn_aggr(moments[:], stats[:].rearrange("p a b -> p (a b)")).then_inc(moments_ready, 1)
                dve.wait_ge(moments_ready, n + 1)
                until(dve, rstd_ready, n)
                dve.tensor_scalar(var_eps[:], moments[:, 1:2], EPS, XS ** -2, ALU.add, ALU.mult)\
                   .then_inc(var_ready, 1)

            def normalise(n, slot):
                dve.wait_ge(rstd_ready, n + 1)
                dve.tensor_scalar(xn[:, slot], xn[:, slot], moments[:, 0:1], rstd[:, 0:1],
                                  ALU.subtract, ALU.mult).then_inc(xn_ready, 1)

            def power_of_two(largest, scale, inv, chain, before):
                wide = largest.shape[-1]
                dve.tensor_scalar(binade[:, 0, 0:wide].bitcast(I32), largest.bitcast(I32), 0x7f800000, None,
                                  ALU.bitwise_and).then_inc(chain, 1)
                dve.wait_ge(chain, before + 1)
                dve.tensor_scalar(binade[:, 1, 0:wide], binade[:, 0, 0:wide], 2.0 ** -100, None, ALU.max)\
                   .then_inc(chain, 1)
                dve.wait_ge(chain, before + 2)
                dve.reciprocal(scale, binade[:, 1, 0:wide]).then_inc(chain, 1)
                dve.wait_ge(chain, before + 3)
                apart(dve, dve_passed)
                dve.tensor_scalar(inv, binade[:, 1, 0:wide], 1 / TOP, None, ALU.mult).then_inc(chain, 1)
                dve.tensor_scalar(scale, scale, TOP, None, ALU.mult).then_inc(chain, 1)
                dve.wait_ge(chain, before + 5)

            def ctx_maximum(n):
                dve.wait_ge(ctx_loaded, 16 * (n + 1))
                until(dve, ctx_all_max_ready, n)
                dve.tensor_reduce(ctx_max[:], ctx_raw[:].rearrange("p k t -> p (k t)"), AX, ALU.max,
                                  apply_absolute_value=True).then_inc(ctx_max_ready, 1)

            def ctx_scaling(n):
                dve.wait_ge(ctx_all_max_ready, n + 1)
                until(dve, ctx_hi_ready, n)
                power_of_two(ctx_all_max[:], ctx_scale[:], ctx_inv[:], ctx_chain, 6 * n)

            def kv_unscaling(slot):
                dve.tensor_scalar(kv_inv[:, slot], w_inv[:, :, 1:3], ctx_inv[:, 0:1], None, ALU.mult)\
                   .then_inc(ctx_chain, 1)

            def ctx_low(n, slot):
                dve.wait_ge(ctx_hi_ready, n + 1)
                dve.scalar_tensor_tensor(out=ctx_lo[:, slot], in0=ctx_raw[:], scalar=ctx_scale[:, 0:1],
                                         in1=ctx_hi[:, slot], op0=ALU.mult, op1=ALU.subtract).then_inc(ctx_lo_ready, 1)

            def low_xn(n, slot, j):
                dve.wait_ge(xn_hi_ready, n + 1)
                dve.tensor_tensor(xn_lo[:, slot, j], XT_ps, xn_hi[:, slot, j], ALU.subtract).then_inc(xn_lo_ready, 1)

            def maximum(j, g, load):
                for m in range(3):
                    dve.wait_ge(w_loaded[3 * g + m], 16 * load)
                dve.tensor_reduce(w_part_max[:], w_raw[g], AX, ALU.max, apply_absolute_value=True)\
                   .then_inc(w_max_ready, 1)

            def scaling(j, g):
                dve.wait_ge(w_all_max_ready, j + 1)
                dve.tensor_scalar(w_bound[:], w_all_max[:], fold_growth[:, 0:1], None, ALU.mult).then_inc(w_chain, 1)
                dve.wait_ge(w_chain, 6 * j + 1)
                power_of_two(w_bound[:], w_scale[:, g], w_inv_flat[:, at3(j)], w_chain, 6 * j + 1)

            def low(j, g):
                dve.wait_ge(w_hi_ready, 3 * j + 1)
                apart(dve, dve_passed)
                dve.scalar_tensor_tensor(out=w_lo[:, 0, :, at(j)], in0=W_ps[0], scalar=w_scale[:, g, 0:1],
                                         in1=w_hi[:, 0, :, at(j)], op0=ALU.mult, op1=ALU.subtract)\
                   .then_inc(wq_lo_ready, 1)

            maximum(0, 0, 1)
            scaling(0, 0)
            moments_of(0, 0)
            normalise(0, 0)
            maximum(1, 1, 1)
            low(0, 0)
            ctx_maximum(0)
            dve.wait_ge(xn_hi_ready, KT)
            dve.tensor_tensor(xn_lo[:, 0].rearrange("p k t -> p (k t)"), X0_ps,
                              xn_hi[:, 0].rearrange("p k t -> p (k t)"), ALU.subtract).then_inc(xn_lo_ready, KT)
            ctx_scaling(0)
            with dve.Fori(0, (KT - 2) // 3) as i:
                for g in range(3):
                    j = 3 * i + 1 + g
                    scaling(j, (1 + g) % 3)
                    maximum(j + 1, (2 + g) % 3, i + (2 if g else 1))
                    low(j, (1 + g) % 3)
            scaling(KT - 1, (KT - 1) % 3)
            ctx_low(0, 0)
            dve.wait_ge(xn_ready, 1)
            moments_of(1, 1)
            normalise(1, 1)
            dve.wait_ge(w_chain, 6 * KT)
            dve.tensor_scalar(q_inv[:], w_inv[:, :, 0], 1 / XS, None, ALU.mult).then_inc(q_inv_ready, 1)
            kv_unscaling(0)
            low(KT - 1, (KT - 1) % 3)
            dve.wait_ge(wq_lo_ready, KT)
            dve.wait_ge(wkv_lo_ready, 2 * KT + 2)

            def steps(base, batch, ts):
                for t in ts:
                    s, b, j = base + t, batch + t // KT, t % KT
                    if t < 16:
                        dve.wait_ge(qk_kept, 2 * s + 2)
                        until(dve, v_split, s - 1)
                        dve.scalar_tensor_tensor(out=v_f[:, t % 2], in0=QKV_ps[:, t % 2, 2 * P:3 * P],
                                                 scalar=kv_inv[:, t // KT, j, 1:2], in1=bias_v[:, j * P:(j + 1) * P],
                                                 op0=ALU.mult, op1=ALU.add).then_inc(v_kept, 1)
                        if not (isinstance(b, int) and b + 1 >= NB):
                            low_xn(s + KT, (t // KT + 1) % 2, j)
                        dve.wait_ge(qk_hi_ready, s + 1)
                        until(dve, scored, s - 1)
                        dve.tensor_tensor(qk_lo[:, t % 2], qk_f[:, t % 2], qk_hi[:, t % 2].bitcast(F32), ALU.subtract)\
                           .then_inc(qk_lo_ready, 1)
                        dve.tensor_tensor(k_wide_hi[:, t % 2],
                                          qk_hi[:, t % 2, 1].bitcast(F32).unsqueeze(1).to_broadcast([P, PAIRS, P]),
                                          pair_mask[:].unsqueeze(2).to_broadcast([P, PAIRS, P]), ALU.mult)\
                           .then_inc(k_wide_hi_ready, 1)
                        if not (isinstance(b, int) and b + 1 >= NB):
                            if j == 1:
                                ctx_maximum(b + 1)
                            if j == 2:
                                ctx_scaling(b + 1)
                                kv_unscaling((t // KT + 1) % 2)
                            if j == 4:
                                ctx_low(b + 1, (t // KT + 1) % 2)
                    if t == 16:
                        split_ot(dve, 0)
                        split_wo(dve, range(1))
                    r = s - 1
                    if not (isinstance(r, int) and r < 0) and t < 17:
                        dve.wait_ge(scored, r + 1)
                        until(dve, sm_ready, r - 1)
                        dve.tensor_reduce(neg_max[:, (t - 1) % 2], S_pairs, AX, ALU.max, negate=True)\
                           .then_inc(max_ready, 1)
                        dve.wait_ge(max_ready, r + 1)
                        until(dve, s_transposed, r - 1)
                        dve.tensor_tensor(s_m[:, (t - 1) % 2], S_pairs,
                                          neg_max[:, (t - 1) % 2].unsqueeze(2).to_broadcast([P, PAIRS, P]),
                                          ALU.add).then_inc(sm_ready, 1)
                    r = s - 3
                    if not (isinstance(r, int) and r < 0) and t < 19:
                        w = (t - 3) % 2
                        dve.wait_ge(attended, r + 1)
                        until(dve, o_ready, r - 1)
                        dve.tensor_reduce(o_sum[:, w], PV_pairs[:, :, 0:3 * DK].rearrange("p c (q d) -> p c d q", q=3),
                                          AX, ALU.add).then_inc(o_summed, 1)
                        dve.reciprocal(r_den[:, w], PV_pairs[:, :, VP - 1:VP]).then_inc(den_ready, 1)
                        dve.wait_ge(o_summed, r + 1)
                        dve.wait_ge(den_ready, r + 1)
                        until(dve, o_transposed, r - 1)
                        dve.tensor_tensor(o_tok[:, w].rearrange("p (c d) -> p c d", d=DK), o_sum[:, w],
                                          r_den[:, w].to_broadcast([P, PAIRS, DK]), ALU.mult).then_inc(o_ready, 1)
                    if t == 16:
                        split_wo(dve, range(1, 4))
                    if t == 17:
                        split_wo(dve, range(4, 6))
                    if t == 18:
                        split_wo(dve, range(6, KT))
                        split_ot(dve, 1)
                    if t < 16 and not (isinstance(b, int) and b + 2 >= NB):
                        if j == 3:
                            moments_of(b + 2, t // KT)
                        if j == 6:
                            normalise(b + 2, t // KT)

            steps(0, 0, range(16))
            with dve.Fori(1, NB // 2 - 1) as i:
                steps(i * 16, i * 2, range(16))
            steps(STEPS - 16, NB - 2, range(19))

        @block.tensor
        def _(pe):
            pe.wait_ge(const_loaded, 16 * 4)
            pe.wait_ge(fold_ready, KT)
            for j in range(KT):
                pe.matmul(QKV_ps[:, 0, 2 * j:2 * j + 2], fold[:, at(j)], bqk_raw[:, j, :], start=True, stop=True)
            pe.wait_ge(bv_wide_ready, 1)
            for j in range(KT):
                mm = pe.matmul(banks[3][:, j // 4, (j % 4) * P:(j % 4 + 1) * P], bv_wide[:, j, :], fold[:, at(j)],
                               start=True, stop=True)
            mm.then_inc(bias_made, 1)

            def tiles(j, g, load=1):
                for m in range(3):
                    pe.wait_ge(w_loaded[3 * g + m], 16 * load)
                    if isinstance(j, int) and j == 0 and m == 2:
                        pe.wait_ge(bias_ready, 1)
                    until(pe, *((w_s_ready, 2 * (j - 1) + m) if m else (wq_lo_ready, j)))
                    apart(pe, pe_passed)
                    for k in range(KT):
                        mm = pe.matmul(W_ps[m][:, k, :], w_raw[g][:, m, k * P:(k + 1) * P],
                                       fold[:, at(j)], start=True, stop=True)
                    mm.then_inc(w_folded, 1)

            tiles(0, 0)
            pe.wait_ge(xn_ready, 1)
            pe.wait_ge(bias_ready, 2)
            for k in range(KT):
                mm = pe.transpose(X0_ps[:, at(k)], xn[:, 0, at(k)], ident[:])
            mm.then_inc(xn_transposed, KT)
            tiles(1, 1)
            other_tiles(pe, tiles)
            pe.wait_ge(w_s_ready, 2 * KT)
            pe.wait_ge(wq_lo_ready, KT)

            def transpose_xn(n, slot, j):
                until(pe, xn_lo_ready, n)
                until(pe, o_t_kept, n - KT - 4)
                pe.transpose(XT_ps, xn[:, slot, j * P:(j + 1) * P], ident[:]).then_inc(xn_transposed, 1)

            def fill(place):
                for k in {(16, 1): (0,), (17, 0): (1, 2, 3), (17, 1): (4,), (18, 0): (5,), (18, 1): (6, 7)}.get(place, ()):
                    if k == 0:
                        pe.wait_ge(v_kept, STEPS)
                        pe.wait_ge(ot_lo_ready, 1)
                    pe.wait_ge(wo_lo_ready, k + 1)
                    mm = project_out(pe, 0, k)
                    if k == KT - 1:
                        mm.then_inc(o_projected, 1)

            def steps(base, batch, ts):
                for t in ts:
                    s, b, j = base + t, batch + t // KT, t % KT
                    here = t // KT % 2
                    r = s - 5
                    if not (isinstance(r, int) and r < 0):
                        pe.wait_ge(o_ready, r + 1)
                        until(pe, o_t_kept, r)
                        if not (isinstance(r, int) and s + KT > STEPS):
                            pe.wait_ge(xn_lo_ready, s + KT)
                        pe.transpose(OT_ps, o_tok[:, (t - 5) % 2], ident[:]).then_inc(o_transposed, 1)
                    if t < 16:
                        if j == 0:
                            pe.wait_ge(xn_lo_ready, KT * (b + 1))
                            pe.wait_ge(ctx_lo_ready, b + 1)
                        if isinstance(b, int) and b == 0:
                            pe.wait_ge(wkv_lo_ready, 2 * (j + 2))
                        cols = slice(j * P, (j + 1) * P)
                        until(pe, v_kept, s - 1)
                        for m, (src_hi, src_lo) in enumerate(((xn_hi, xn_lo), (ctx_hi, ctx_lo), (ctx_hi, ctx_lo))):
                            for k in range(KT):
                                for src, w in ((src_hi, w_hi), (src_lo, w_hi), (src_hi, w_lo)):
                                    act_tile, w_tile = src[:, here, k], w[:, m, k, cols]
                                    mm = pe.matmul(QKV_ps[:, t % 2, m * P:(m + 1) * P],
                                                   w_tile if m < 2 else act_tile, act_tile if m < 2 else w_tile,
                                                   start=(k == 0 and src is src_hi and w is w_hi),
                                                   stop=(k == KT - 1 and w is w_lo))
                        mm.then_inc(projected, 1)
                        if not (isinstance(b, int) and b + 1 >= NB):
                            if j == 0:
                                pe.wait_ge(xn_ready, b + 2)
                            transpose_xn(s + KT, 1 - here, j)
                    r = s - 1
                    if not (isinstance(r, int) and r < 0) and t < 17:
                        pe.wait_ge(k_wide_hi_ready, r + 1)
                        pe.wait_ge(k_wide_lo_ready, r + 1)
                        until(pe, sm_ready, r)
                        for q, k_wide in ((qk_hi, k_wide_hi), (qk_lo, k_wide_hi), (qk_hi, k_wide_lo)):
                            for h in range(2):
                                mm = pe.matmul(S_ps[:, h], q[:, (t - 1) % 2, 0],
                                               k_wide[:, (t - 1) % 2, 4 * h:4 * h + 4].rearrange("p c k -> p (c k)"),
                                               start=(q is qk_hi and k_wide is k_wide_hi), stop=(k_wide is k_wide_lo))
                        mm.then_inc(scored, 1)
                    r = s - 2
                    if not (isinstance(r, int) and r < 0) and t < 18:
                        pe.wait_ge(sm_ready, r + 1)
                        until(pe, e_ready, r)
                        for c in range(PAIRS):
                            mm = pe.transpose(T_pairs[:, c, :], s_m[:, t % 2, c, :], ident[:])
                        mm.then_inc(s_transposed, 1)
                    fill((t, 0))
                    r = s - 3
                    if not (isinstance(r, int) and r < 0) and t < 19:
                        pe.wait_ge(e_hi_ready, r + 1)
                        pe.wait_ge(e_lo_ready, r + 1)
                        pe.wait_ge(v_split, r + 1)
                        if isinstance(r, int) and r == 0:
                            pe.wait_ge(ones_ready, 1)
                        until(pe, o_summed, r)
                        until(pe, den_ready, r)
                        for c in range(PAIRS):
                            for e in (e_hi, e_lo):
                                mm = pe.matmul(PV_pairs[:, c, :], e[:, (t - 3) % 2, c, :],
                                               v_parts[:, (t - 3) % 4, c, 0:VP], start=(e is e_hi), stop=(e is e_lo))
                        mm.then_inc(attended, 1)
                    fill((t, 1))

            steps(0, 0, range(16))
            with pe.Fori(1, NB // 2 - 1) as i:
                steps(i * 16, i * 2, range(16))
            steps(STEPS - 16, NB - 2, range(21))

        ab_scope.close()

        c_block = ExitStack()
        block = c_block.enter_context(nc.Block())
        X2_ps = banks[1][:].rearrange("p b (k t) -> p (b k) t", t=P)
        xh_b = xh[:].rearrange("p k (b t) -> p k b t", t=P)
        xl_b = xl[:].rearrange("p k (b t) -> p k b t", t=P)

        def pairs_of_batches(eng, steps, tail):
            steps(0, range(2))
            with eng.Fori(1, NB // 2) as i:
                steps(i * 2, range(2))
            steps(NB - 2, range(2, 2 + tail))

        @block.sync
        def _(sp):
            sp.dma_start(bo_rows[:], b_o.partition_broadcast(P)).then_inc(bo_loaded, 16)

            def steps(base, ts):
                for t in ts:
                    b, q = base + t, t % 2
                    if t < 2:
                        if not isinstance(b, int):
                            sp.wait_ge(ot_lo_ready, b - 1)
                            sp.dma_start(ot_in[:, q], ot_scratch[b].rearrange("p k t -> p (k t)"))\
                              .then_inc(ot_loaded[q], 16)
                        until(sp, x1_ready, b - 1)
                        sp.dma_start(x_again[:, q], x[b]).then_inc(xa_loaded[q], 16)
                    if real(b - 2):
                        sp.wait_ge(x1_ready, b - 1)
                        sp.dma_start(x1_scratch[b - 2], x1[:, q]).then_inc(x1_stored[q], 16)

            def first_of_d():
                sp.dma_start(g_s[:], gate_s).then_inc(scales_loaded, 16)
                sp.dma_start(u_s[:], up_s).then_inc(scales_loaded, 16)
                sp.wait_ge(wo_lo_ready, KT)
                for c in range(4):
                    until(sp, gu_ready, c - 1)
                    sp.dma_start(gu_raw[:, c % 2], (gate_w, up_w)[c // 2][c % 2].rearrange("p k f -> p (k f)"))\
                      .then_inc(gu_loaded[c % 2], 16)

            pairs_of_batches(sp, steps, 0)
            first_of_d()
            steps(NB - 2, range(2, 4))
            for q in range(2):
                sp.wait_ge(x1_stored[q], 16 * NB // 2)

        @block.gpsimd
        def _(pool):
            pool.memset(c_half[:], -0.5).then_inc(c_half_ready, 1)
            pool.wait_ge(c_half_ready, 1)
            pool.wait_ge(bo_loaded, 16)

            def steps(base, ts):
                for t in ts:
                    b, q = base + t, t % 2
                    if t < 2:
                        pool.wait_ge(xa_loaded[q], 8 * (b - q) + 16)
                        pool.tensor_tensor(x_again[:, q], x_again[:, q], bo_rows[:], ALU.add).then_inc(xb_ready, 1)
                    if real(b - 1):
                        pool.wait_ge(c_var_ready, b)
                        pool.tensor_tensor(c_rstd[:], c_var[:], c_half[:], ALU.pow).then_inc(c_rstd_ready, 1)

            pairs_of_batches(pool, steps, 1)

        @block.scalar
        def _(act):
            def steps(base, ts):
                for t in ts:
                    b, q = base + t, t % 2
                    if t < 2 and not isinstance(b, int):
                        act.wait_ge(ot_loaded[q], 8 * (b - q) + 16)
                        until(act, o_projected, b - 1)
                        act.activation(ot_hi[:, q], ot_in[:, q], ACT.Copy).then_inc(ot_hi_ready, 1)
                    if real(b - 2):
                        act.wait_ge(xn2_transposed, b - 1)
                        apart(act, act_passed)
                        act.activation(xh_b[:, :, b - 2, :], X2_ps, ACT.Copy).then_inc(xh_ready, 1)

            pairs_of_batches(act, steps, 0)
            for c in range(4):
                act.wait_ge(gu_loaded[c % 2], 16 * (c // 2 + 1))
                act.activation(gu_w[0][:, c // 2, c % 2].rearrange("p k f -> p (k f)"), gu_raw[:, c % 2], ACT.Copy)\
                   .then_inc(gu_ready, 1)
            steps(NB - 2, range(2, 4))

        @block.vector
        def _(dve):
            def steps(base, ts):
                for t in ts:
                    b, q = base + t, t % 2
                    if t < 2 and not isinstance(b, int):
                        dve.wait_ge(ot_hi_ready, b + 1)
                        until(dve, o_projected, b - 1)
                        dve.tensor_tensor(ot_lo[:, q], ot_in[:, q], ot_hi[:, q].bitcast(F32), ALU.subtract)\
                           .then_inc(ot_lo_ready, 1)
                    if real(b - 2):
                        dve.wait_ge(xh_ready, b - 1)
                        dve.tensor_tensor(xl_b[:, :, b - 2, :], X2_ps, xh_b[:, :, b - 2, :], ALU.subtract)\
                           .then_inc(xl_ready, 1)
                    if real(b - 1) and t < 3:
                        r, w = b - 1, (t - 1) % 2
                        dve.wait_ge(o_projected, r + 1)
                        dve.wait_ge(xb_ready, r + 1)
                        until(dve, x1_stored[w], 8 * (r - w))
                        dve.tensor_tensor(x1[:, w], O_ps[w], x_again[:, w], ALU.add).then_inc(x1_ready, 1)
                        dve.wait_ge(x1_ready, r + 1)
                        for h in range(2):
                            dve.bn_stats(c_stats[:, h], x1[:, w, h * 512:(h + 1) * 512]).then_inc(c_stats_ready, 1)
                        dve.wait_ge(c_stats_ready, 2 * r + 2)
                        apart(dve, dve_passed)
                        dve.bn_aggr(c_moments[:], c_stats[:].rearrange("p a b -> p (a b)")).then_inc(c_moments_ready, 1)
                        dve.wait_ge(c_moments_ready, r + 1)
                        dve.tensor_scalar(c_var[:], c_moments[:, 1:2], EPS, XS ** -2, ALU.add, ALU.mult)\
                           .then_inc(c_var_ready, 1)
                        dve.wait_ge(c_rstd_ready, r + 1)
                        until(dve, xn2_transposed, r)
                        dve.tensor_scalar(xn2[:, 0], x1[:, w], c_moments[:, 0:1], c_rstd[:, 0:1],
                                          ALU.subtract, ALU.mult).then_inc(xn2_ready, 1)

            pairs_of_batches(dve, steps, 2)

        @block.tensor
        def _(pe):
            def steps(base, ts):
                for t in ts:
                    b, q = base + t, t % 2
                    if t < 2 and not (isinstance(b, int) and b == 0):
                        pe.wait_ge(ot_lo_ready, b + 1)
                        until(pe, x1_ready, b - 1)
                        for j in range(KT):
                            mm = project_out(pe, q, j)
                        mm.then_inc(o_projected, 1)
                    if isinstance(b, int) and b == NB:
                        pe.wait_ge(gu_ready, 4)
                        pe.wait_ge(xl_ready, TPC)
                        for f in range(FB):
                            up_or_gate(pe, G_ps, 0, f, 0, slice(0, CH)).then_inc(gated, 1)
                    if real(b - 1):
                        pe.wait_ge(xn2_ready, b)
                        until(pe, xl_ready, b - 1)
                        for k in range(KT):
                            mm = pe.transpose(X2_ps[:, k], xn2[:, 0, k * P:(k + 1) * P], ident[:])
                        mm.then_inc(xn2_transposed, 1)

            pairs_of_batches(pe, steps, 1)

        c_block.close()

        d_block = ExitStack()
        block = d_block.enter_context(nc.Block())
        D_ps = [banks[2][:, 0], banks[2][:, 1], banks[3][:, 0], banks[3][:, 1]]
        UPC = FB
        DPC = 2 * TPC
        SPB = NCH
        LAST = NBLK - 2

        def column(table, n):
            return table[:, n:n + 1] if isinstance(n, int) else table[:, bass.ds(n, 1)]

        def pairs_of_blocks(eng, steps):
            steps(0, 0)
            with eng.Fori(1, NBLK // 2 - 1) as i:
                steps(i * 2 * SPB, i * 2)
            steps(LAST * SPB, LAST)

        @block.sync
        def _(sp):
            sp.dma_start(ds_rows[:], down_s.partition_broadcast(P)).then_inc(scales_loaded, 16)

            for f in range(2):
                sp.dma_start(d_raw[:, f], down_w[f]).then_inc(d_loaded[f], 16)

            def load_gu(a, kind, tile, q):
                until(sp, gu_ready, a - 1)
                sp.dma_start(gu_raw[:, q], (gate_w, up_w)[kind][tile].rearrange("p k f -> p (k f)"))\
                  .then_inc(gu_loaded[q], 16)

            def load_d(a, tile, q):
                until(sp, d_ready, a - 1)
                sp.dma_start(d_raw[:, q], down_w[tile]).then_inc(d_loaded[q], 16)

            def steps(base, block0):
                for n in range(2):
                    nxt = block0 + n + 1
                    if isinstance(nxt, int) and nxt >= NBLK:
                        continue
                    for c in range(4):
                        load_gu(nxt * 4 + c, c // 2, nxt * 2 + c % 2, c % 2)
                        if c % 2:
                            load_d(nxt * 2 + c // 2, nxt * 2 + c // 2, c // 2)

            pairs_of_blocks(sp, steps)
            sp.wait_ge(gu_ready, 4 * NBLK)
            sp.wait_ge(d_ready, 2 * NBLK)
            for tile in range(NB + 4):
                if tile >= 4:
                    sp.wait_ge(y_ready, 2 * (tile - 3))
                if tile < NB:
                    sp.dma_start(x1_in[:, tile % 4], x1_scratch[tile]).then_inc(x1_loaded[tile % 4], 16)
                if tile >= 4:
                    sp.dma_start(out[tile - 4], acc[:, tile - 4]).then_inc(y_stored, 16)
            sp.wait_ge(y_stored, 16 * NB)

        @block.gpsimd
        def _(pool):
            def steps(base, block0):
                for t in range(2 * SPB):
                    r = base + t
                    for f in range(FB):
                        u = r * UPC + f
                        pool.wait_ge(h_hi_ready, u + 1)
                        until(pool, downed, (r - 1) * DPC)
                        pool.tensor_tensor(h_lo[:, t % 2, f], h_f[:, f % 2], h_hi[:, t % 2, f].bitcast(F32),
                                           ALU.subtract).then_inc(h_lo_ready, 1)
                    if isinstance(r, int) and r > LAST * SPB + SPB:
                        scale(t - SPB - 1)
                if isinstance(base, int) and base > 0:
                    scale(SPB - 1)

            def scale(c):
                for v in range(DPC):
                    tile, h = c * TPC + v // 2, slice(v % 2 * 512, v % 2 * 512 + 512)
                    pool.wait_ge(acc_added, ((NBLK - 1) * SPB + c) * DPC + v + 1)
                    pool.tensor_tensor(acc[:, tile, h], acc[:, tile, h], ds_rows[:, h], ALU.mult).then_inc(acc_scaled, 1)

            pool.wait_ge(scales_loaded, 48)
            pairs_of_blocks(pool, steps)

        @block.scalar
        def _(act):
            def convert(a, c, buf, before):
                act.wait_ge(gu_loaded[c % 2], 8 * (a - c % 2) + 16)
                until(act, upped, before)
                act.activation(gu_w[buf][:, c // 2, c % 2].rearrange("p k f -> p (k f)"), gu_raw[:, c % 2],
                               ACT.Copy).then_inc(gu_ready, 1)

            act.wait_ge(scales_ready, 2)

            def steps(base, block0):
                for t in range(2 * SPB):
                    r, n, c = base + t, block0 + t // SPB, t % SPB
                    for f in range(FB):
                        u = r * UPC + f
                        act.wait_ge(gated, u + 1)
                        until(act, h_ready, u - 1)
                        apart(act, act_passed)
                        act.activation(silu[:, f % 2], G_ps[:, f % 2], ACT.Silu,
                                       scale=column(g_sx, n * FB + f)).then_inc(silu_ready, 1)
                        act.wait_ge(h_ready, u + 1)
                        until(act, downed, (r - 1) * DPC)
                        act.activation(h_hi[:, t % 2, f], h_f[:, f % 2], ACT.Copy).then_inc(h_hi_ready, 1)
                    if not (isinstance(n, int) and n + 1 >= NBLK):
                        convert((n + 1) * 4 + c, c, (t // SPB + 1) % 2, n * SPB * UPC)

            pairs_of_blocks(act, steps)

        @block.vector
        def _(dve):
            dve.wait_ge(scales_loaded, 48)
            dve.tensor_scalar(g_sx[:], g_s[:], 1 / XS, None, ALU.mult).then_inc(scales_ready, 1)
            dve.tensor_scalar(u_sx[:], u_s[:], 1 / XS, None, ALU.mult).then_inc(scales_ready, 1)

            def convert(a, f, buf, before):
                dve.wait_ge(d_loaded[f], 8 * (a - f) + 16)
                until(dve, downed, before)
                dve.tensor_copy(d_w[:, buf, f], d_raw[:, f]).then_inc(d_ready, 1)

            for f in range(FB):
                convert(f, f, 0, 0)
            dve.wait_ge(scales_ready, 2)

            def add(r, c):
                for v in range(DPC):
                    tile, h = c * TPC + v // 2, slice(v % 2 * 512, v % 2 * 512 + 512)
                    dve.wait_ge(downed, r * DPC + v + 1)
                    if isinstance(r, int) and r < SPB:
                        dve.tensor_copy(acc[:, tile, h], D_ps[v % 4]).then_inc(acc_added, 1)
                    else:
                        dve.tensor_tensor(acc[:, tile, h], D_ps[v % 4], acc[:, tile, h], ALU.add)\
                           .then_inc(acc_added, 1)
                    if isinstance(r, int) and r >= (NBLK - 1) * SPB and v >= 2:
                        residual(c, v - 2)
                if isinstance(r, int) and r >= (NBLK - 1) * SPB:
                    residual(c, DPC - 2)
                    residual(c, DPC - 1)

            def residual(c, v):
                tile, h = c * TPC + v // 2, slice(v % 2 * 512, v % 2 * 512 + 512)
                dve.wait_ge(acc_scaled, c * DPC + v + 1)
                dve.wait_ge(x1_loaded[tile % 4], 16 * (tile // 4 + 1))
                dve.tensor_tensor(acc[:, tile, h], acc[:, tile, h], x1_in[:, tile % 4, h], ALU.add).then_inc(y_ready, 1)

            def steps(base, block0):
                for t in range(2 * SPB):
                    r, n, c = base + t, block0 + t // SPB, t % SPB
                    for f in range(FB):
                        u = r * UPC + f
                        dve.wait_ge(upped, u + 1)
                        dve.wait_ge(silu_ready, u + 1)
                        until(dve, h_lo_ready, u - 1)
                        dve.scalar_tensor_tensor(out=h_f[:, f % 2], in0=U_ps[:, f % 2], scalar=column(u_sx, n * FB + f),
                                                 in1=silu[:, f % 2], op0=ALU.mult, op1=ALU.mult).then_inc(h_ready, 1)
                    if real(r - 1):
                        add(r - 1, (t - 1) % SPB)
                    if c % 2 and not (isinstance(n, int) and n + 1 >= NBLK):
                        convert((n + 1) * 2 + c // 2, c // 2, (t // SPB + 1) % 2, n * SPB * DPC)
                if isinstance(base, int) and base > 0:
                    add(base + 2 * SPB - 1, SPB - 1)

            pairs_of_blocks(dve, steps)

        @block.tensor
        def _(pe):
            def down(r, c, buf, slot):
                pe.wait_ge(h_lo_ready, r * UPC + UPC)
                for v in range(DPC):
                    until(pe, acc_added, r * DPC + v - 3)
                    for f in range(FB):
                        for part in (h_hi, h_lo):
                            mm = pe.matmul(D_ps[v % 4], part[:, slot, f, v // 2 * P:(v // 2 + 1) * P],
                                           d_w[:, buf, f, v % 2 * 512:v % 2 * 512 + 512],
                                           start=(f == 0 and part is h_hi), stop=(f == FB - 1 and part is h_lo))
                    mm.then_inc(downed, 1)

            def steps(base, block0):
                for t in range(2 * SPB):
                    r, n, c, buf = base + t, block0 + t // SPB, t % SPB, t // SPB
                    if c == 0:
                        pe.wait_ge(gu_ready, n * 4 + 4)
                    tokens = slice(c * CH, (c + 1) * CH)
                    for f in range(FB):
                        u = r * UPC + f
                        for kind, (bank, done, free) in enumerate(((G_ps, gated, silu_ready), (U_ps, upped, h_ready))):
                            if isinstance(r, int) and r == 0 and kind == 0:
                                continue
                            until(pe, free, u - 1)
                            up_or_gate(pe, bank, kind, f, buf, tokens).then_inc(done, 1)
                    if real(r - 1):
                        if c == 1:
                            pe.wait_ge(d_ready, n * 2 + 2)
                        down(r - 1, (c - 1) % SPB, (t - 1) // SPB % 2, (t - 1) % 2)
                if isinstance(base, int) and base > 0:
                    down(base + 2 * SPB - 1, SPB - 1, 1, 1)

            pairs_of_blocks(pe, steps)

        d_block.close()


def kernel(**inputs):
    import numpy as np
    import concourse.bacc as bacc
    from concourse.bass_utils import run_bass_kernel_spmd

    a = {n: np.asarray(v) for n, v in inputs.items()}

    def tiled(w):
        return w.reshape(-1, P, w.shape[1])

    def transposed_tiles(w):
        return w.reshape(FT, P, KT, P).transpose(0, 3, 2, 1)

    row = np.arange(P)
    pair_d = row // STATES
    arrays = {
        "x": a["x"],
        "ctx_t": a["ctx_4096"].reshape(NB, P, KT, P).transpose(0, 3, 2, 1),
        "wqkv": np.stack([tiled(a[f"L0_xattn_W{c}"]) for c in "qkv"], 1).reshape(3 * KT, P, D),
        "b_qk": np.stack([a["L0_xattn_bq"], a["L0_xattn_bk"]], -1).reshape(KT, P, 2).transpose(1, 0, 2),
        "b_v": a["L0_xattn_bv"].reshape(KT, P).T,
        "mix_rows": np.repeat(a["L0_xattn_interference"][:, None], DK, 1).reshape(KT, P, STATES).transpose(1, 0, 2),
        "amp": a["L0_xattn_amp"],
        "wo_t": a["L0_xattn_Wo"].T.reshape(HEADS, DK, STATES, D).transpose(0, 2, 1, 3).reshape(KT, P, D),
        "b_o": a["L0_xattn_bo"],
        "gate_w": transposed_tiles(a["L0_ffn_gate_wq"]),
        "gate_s": a["L0_ffn_gate_scale"].reshape(FT, P).T,
        "up_w": transposed_tiles(a["L0_ffn_up_wq"]),
        "up_s": a["L0_ffn_up_scale"].reshape(FT, P).T,
        "down_w": a["L0_ffn_down_wq"].T.reshape(FT, P, D),
        "down_s": a["L0_ffn_down_scale"],
        "ident_c": np.eye(P, dtype=np.float32),
        "pair_mask_c": (row[:, None] // DK == np.arange(PAIRS)).astype(np.float32),
        "fold_mask_c": (pair_d[:, None] == np.arange(HT * DK)).astype(np.float32).reshape(P, HT, DK),
        "state_eye_c": (row[:, None] % STATES == np.arange(STATES)).astype(np.float32),
    }
    nc = bacc.Bacc("TRN2", target_bir_lowering=False, num_devices=1)
    arrays = {n: np.ascontiguousarray(v) for n, v in arrays.items()}
    handles = {n: nc.dram_tensor(n, v.shape, mybir.dt.from_np(v.dtype), kind="ExternalInput").ap()
               for n, v in arrays.items()}
    out = nc.dram_tensor("out", (NB, P, D), F32, kind="ExternalOutput").ap()
    program(nc, out=out, **handles)
    result = run_bass_kernel_spmd(nc, [arrays], core_ids=[0])
    return result.results[0]["out"]
```
